# Optimizing a Trainium2 kernel written in Bass

```python
import numpy as np
import jax
import jax.numpy as jnp

def _softmax(x, axis=-1):
    return jax.nn.softmax(x, axis=axis)

def _gelu(x):
    return jax.nn.gelu(x, approximate=True)

def _silu(x):
    return jax.nn.silu(x)

def _sigmoid(x):
    return jax.nn.sigmoid(x)

def _layernorm(x, axis=-1, eps=1e-05):
    m = jnp.mean(x, axis=axis, keepdims=True)
    v = jnp.var(x, axis=axis, keepdims=True)
    return (x - m) / jnp.sqrt(v + eps)

def _scatter_add(tgt, idx, src, axis=0):
    return tgt.at[idx].add(src)

def _segment_sum(src, seg, n):
    return jax.ops.segment_sum(src, seg, n)
kernel_name = 'mk_gnn_preln_d1_gnn_r8_a946c1'

def setup_inputs(seed: int=0):
    np.random.seed(seed)
    _w = jnp.asarray

    def _rec_inputs():
        import jax
        import jax.numpy as jnp
        _gk = jax.random.key(seed)
        x = -0.0002117 + 1 * jax.random.normal(jax.random.fold_in(_gk, 1), (12500, 256), jnp.float32)
        _s = jax.random.randint(jax.random.fold_in(_gk, 2), (100000,), 0, 12500, jnp.int32)
        _d = jax.random.randint(jax.random.fold_in(_gk, 3), (100000,), 0, 12500, jnp.int32)
        _loop = jnp.arange(12500, dtype=jnp.int32)
        src = jnp.concatenate([_s, _d, _loop])
        dst = jnp.concatenate([_d, _s, _loop])
        _o = jnp.argsort(dst, stable=True)
        src = src[_o]
        dst = dst[_o]
        return (x, src, dst)
    x, src, dst = _rec_inputs()

    def _L0_gnn_setup():
        import jax, jax.numpy as jnp
        import numpy as np
        N = 12500
        E = 200000
        D = 256
        BN_EPS = 1e-05

        def _batchnorm(x, gamma, beta):
            mu = jnp.mean(x, axis=0)
            var = jnp.var(x, axis=0)
            return (x - mu) * jax.lax.rsqrt(var + BN_EPS) * gamma + beta

        def _gin_conv(x, src, dst, n, W1, b1, gamma, beta, W2, b2):
            agg = jax.ops.segment_sum(x[src], dst, num_segments=n)
            h = x + agg
            h = jax.nn.relu(_batchnorm(h @ W1 + b1, gamma, beta))
            return jax.nn.relu(h @ W2 + b2)
        key = jax.random.key(seed)
        ks = jax.random.split(key, 8)
        x = jax.random.normal(ks[0], (N, D), dtype=jnp.float32)
        edge_index = jax.random.randint(ks[1], (2, E), 0, N, dtype=jnp.int64)
        s = 0.02
        inp = {'x': x, 'edge_index': edge_index, 'g0': jnp.ones((D,), jnp.float32), 'b0': jnp.zeros((D,), jnp.float32), 'W1a': jax.random.normal(ks[2], (D, D), jnp.float32) * s, 'b1a': jnp.zeros((D,), jnp.float32), 'g1': jnp.ones((D,), jnp.float32), 'bt1': jnp.zeros((D,), jnp.float32), 'W1b': jax.random.normal(ks[3], (D, D), jnp.float32) * s, 'b1b': jnp.zeros((D,), jnp.float32), 'W2a': jax.random.normal(ks[4], (D, D), jnp.float32) * s, 'b2a': jnp.zeros((D,), jnp.float32), 'g2': jnp.ones((D,), jnp.float32), 'bt2': jnp.zeros((D,), jnp.float32), 'W2b': jax.random.normal(ks[5], (D, D), jnp.float32) * s, 'b2b': jnp.zeros((D,), jnp.float32)}
        return inp
    _L0_gnn_all = _L0_gnn_setup()
    _L0_gnn_in = {k: v for k, v in _L0_gnn_all.items() if k in ('g0', 'b0', 'W1a', 'b1a', 'g1', 'bt1', 'W1b', 'b1b', 'W2a', 'b2a', 'g2', 'bt2', 'W2b', 'b2b')}
    del _L0_gnn_all
    return {'x': x, 'src': src, 'dst': dst, 'L0_gnn_g0': _L0_gnn_in['g0'], 'L0_gnn_b0': _L0_gnn_in['b0'], 'L0_gnn_W1a': _L0_gnn_in['W1a'], 'L0_gnn_b1a': _L0_gnn_in['b1a'], 'L0_gnn_g1': _L0_gnn_in['g1'], 'L0_gnn_bt1': _L0_gnn_in['bt1'], 'L0_gnn_W1b': _L0_gnn_in['W1b'], 'L0_gnn_b1b': _L0_gnn_in['b1b'], 'L0_gnn_W2a': _L0_gnn_in['W2a'], 'L0_gnn_b2a': _L0_gnn_in['b2a'], 'L0_gnn_g2': _L0_gnn_in['g2'], 'L0_gnn_bt2': _L0_gnn_in['bt2'], 'L0_gnn_W2b': _L0_gnn_in['W2b'], 'L0_gnn_b2b': _L0_gnn_in['b2b']}

def reference(x, src, dst, L0_gnn_g0, L0_gnn_b0, L0_gnn_W1a, L0_gnn_b1a, L0_gnn_g1, L0_gnn_bt1, L0_gnn_W1b, L0_gnn_b1b, L0_gnn_W2a, L0_gnn_b2a, L0_gnn_g2, L0_gnn_bt2, L0_gnn_W2b, L0_gnn_b2b):
    import jax
    import jax.numpy as jnp

    def _L0_gnn_ref(x, edge_index, g0, b0, W1a, b1a, g1, bt1, W1b, b1b, W2a, b2a, g2, bt2, W2b, b2b):
        import jax, jax.numpy as jnp
        import numpy as np
        N = 12500
        E = 200000
        D = 256
        BN_EPS = 1e-05

        def _batchnorm(x, gamma, beta):
            mu = jnp.mean(x, axis=0)
            var = jnp.var(x, axis=0)
            return (x - mu) * jax.lax.rsqrt(var + BN_EPS) * gamma + beta

        def _gin_conv(x, src, dst, n, W1, b1, gamma, beta, W2, b2):
            agg = jax.ops.segment_sum(x[src], dst, num_segments=n)
            h = x + agg
            h = jax.nn.relu(_batchnorm(h @ W1 + b1, gamma, beta))
            return jax.nn.relu(h @ W2 + b2)
        n = x.shape[0]
        src, dst = (edge_index[0], edge_index[1])
        h = _batchnorm(x, g0, b0)
        h = _gin_conv(h, src, dst, n, W1a, b1a, g1, bt1, W1b, b1b)
        h = jax.nn.relu(h)
        h = _gin_conv(h, src, dst, n, W2a, b2a, g2, bt2, W2b, b2b)
        return jax.nn.relu(h)
    edge_index = jnp.stack([src, dst])
    h = jnp.maximum(_layernorm(x, axis=-1), 0.0)
    x = x + _L0_gnn_ref(h, edge_index, L0_gnn_g0, L0_gnn_b0, L0_gnn_W1a, L0_gnn_b1a, L0_gnn_g1, L0_gnn_bt1, L0_gnn_W1b, L0_gnn_b1b, L0_gnn_W2a, L0_gnn_b2a, L0_gnn_g2, L0_gnn_bt2, L0_gnn_W2b, L0_gnn_b2b)
    return x

_drawn_inputs = setup_inputs


def setup_inputs(seed=0):
    import zlib

    import numpy as np

    out = dict(_drawn_inputs(seed))
    spreads = {'L0_gnn_g0': (1.0, 0.2),
     'L0_gnn_b0': (0.0, 0.636),
     'L0_gnn_b1a': (0.0, 2.0),
     'L0_gnn_g1': (1.0, 0.536),
     'L0_gnn_bt1': (0.0, 0.516),
     'L0_gnn_b1b': (0.0, 0.1),
     'L0_gnn_b2a': (0.0, 2.0),
     'L0_gnn_g2': (1.0, 0.2),
     'L0_gnn_bt2': (0.0, 0.532),
     'L0_gnn_b2b': (0.0, 0.1)}
    factors = {}
    for name, (base, spread) in spreads.items():
        noise = np.random.default_rng([zlib.crc32(name.encode()), seed]).standard_normal(out[name].shape)
        drawn = base * np.exp(spread * noise) if base else spread * noise
        out[name] = jnp.asarray(drawn.astype(out[name].dtype))
    for name, factor in factors.items():
        out[name] = (out[name] * factor).astype(out[name].dtype)
    return out
```

```python
from contextlib import ExitStack

import concourse.bass as bass
from concourse import mybir

P = 128
N = 12500
D = 256
E = 212500
KC = D // P
LN_EPS = 1e-5
BN_EPS = 1e-5

NB = (N + P - 1) // P
NPAD = NB * P
LAST = N - (NB - 1) * P
CH = 7
NCH = NB // CH
G = 8
GE = G * P
NG = (E + GE - 1) // GE
TAIL = E - (NG - 1) * GE
NS = NG + NB - 1
R = 4
RW = 272
NC_G = (NG + P - 1) // P

F32 = mybir.dt.float32
I32 = mybir.dt.int32
ALU = mybir.AluOpType
ACT = mybir.ActivationFunctionType


def build(nc, x, src, dst, g0, b0, W1a, b1a, g1, bt1, W1b, b1b, W2a, b2a, g2, bt2, W2b, b2b, out):
    tables = [nc.dram_tensor(f"node_rows_{i}", (NPAD, D), F32, kind="Internal").ap() for i in range(2)]
    layers = [(W1a, b1a, g1, bt1, W1b, b1b), (W2a, b2a, g2, bt2, W2b, b2b)]

    ctx = ExitStack()
    with ctx:
        def sb(name, shape, dt=F32):
            return ctx.enter_context(nc.sbuf_tensor(name, shape, dt))

        def pb(name, shape):
            return ctx.enter_context(nc.psum_tensor(name, shape, F32))

        def sem(name):
            return ctx.enter_context(nc.semaphore(name))

        acc = sb("acc", [P, NB * D])
        degree = sb("degree", [P, NB])
        rows = sb("rows", [P, R * G * RW])
        src_all = sb("src_all", [P, NG * G], I32)
        dst_int = sb("dst_int", [P, NG * G], I32)
        dst_all = sb("dst_all", [P, NG * G])
        src_stage = sb("src_stage", [P, R * G], I32)
        onehot = sb("onehot", [P, 2, G, P])
        iota_row = sb("iota_row", [P, P])
        part_col = sb("part_col", [P, 1])
        ident = sb("ident", [P, P])
        ones = sb("ones", [P, P])
        block_start = sb("block_start", [P, NB])
        block_starts_next = sb("block_starts_next", [P, NB - 1])
        walk_iota = sb("walk_iota", [P, NS])
        group_no = sb("group_no", [P, NC_G])
        group_dst_i = sb("group_dst_i", [P, NC_G], I32)
        group_dst = sb("group_dst", [P, NC_G])
        passed = sb("passed", [P, NB - 1])
        first_block = sb("first_block", [P, NC_G])
        group_step = sb("group_step", [P, NC_G])
        reached = sb("reached", [P, NC_G, NS])
        step_group = sb("step_group", [1, NS], I32)
        step_slot = sb("step_slot", [1, NS], I32)
        group_first_step = sb("group_first_step", [1, NC_G * P], I32)
        w_a = [sb(f"w_a{i}", [P, KC, D]) for i in range(2)]
        w_b = [sb(f"w_b{i}", [P, KC, D]) for i in range(2)]
        vec = sb("vec", [P, 8, KC])
        bias_b = [sb(f"bias_b{i}", [P, D]) for i in range(2)]
        ln_stats = sb("ln_stats", [P, CH, 6])
        ln_mv = sb("ln_mv", [P, 2, CH, 2])
        ln_var = sb("ln_var", [P, 2, CH])
        ln_root = sb("ln_root", [P, 2, CH])
        ln_half = sb("ln_half", [P, CH])
        ln_scale = sb("ln_scale", [P, 2, CH])
        ln_bias = sb("ln_bias", [P, 2, CH])
        bn_stats = sb("bn_stats", [P, KC, NB * 6])
        bn_mv = sb("bn_mv", [P, KC, 2])
        bn_rstd = sb("bn_rstd", [P, KC])
        bn_scale = sb("bn_scale", [P, KC])
        bn_shift = sb("bn_shift", [P, KC])
        bn_var = sb("bn_var", [P, KC])
        bn_root = sb("bn_root", [P, KC])
        bn_half = sb("bn_half", [P, KC])
        diag = sb("diag", [P, 2, KC, P])
        affine_rows = sb("affine_rows", [P, 2, D])
        scaled = sb("scaled", [P, 2, D])
        node_major = sb("node_major", [P, 2, D])
        feat_major = sb("feat_major", [P, 2, KC, P])
        pre_relu = sb("pre_relu", [P, 2, D])

        agg_ps = [pb(f"agg_ps{i}", [P, 512]) for i in range(2)]
        tr_ps = [pb(f"tr_ps{i}", [P, 512]) for i in range(2)]
        mm_ps = [pb(f"mm_ps{i}", [P, 512]) for i in range(2)]
        set_ps = pb("set_ps", [P, 512])

        x_loaded = [sem(f"x_loaded{i}") for i in range(2)]
        edges_loaded = sem("edges_loaded")
        consts_loaded = sem("consts_loaded")
        pool_consts = sem("pool_consts")
        setup_done = sem("setup_done")
        setup_products = sem("setup_products")
        walk_ready = sem("walk_ready")
        ln_step = sem("ln_step")
        waits_passed = sem("waits_passed")
        newton_step = sem("newton_step")
        ln_measured = sem("ln_measured")
        ln_scaled = sem("ln_scaled")
        ln_rooted = sem("ln_rooted")
        bn_rooted = sem("bn_rooted")
        ln_ready = sem("ln_ready")
        h_ready = sem("h_ready")
        table_stored = sem("table_stored")
        src_staged = sem("src_staged")
        slot_landed = [sem(f"slot_landed{i}") for i in range(R)]
        groups_ready = sem("groups_ready")
        groups_free = sem("groups_free")
        onehot_ready = sem("onehot_ready")
        steps_done = sem("steps_done")
        sums_added = sem("sums_added")
        node_major_ready = sem("node_major_ready")
        transposed = sem("transposed")
        transpose_read = sem("transpose_read")
        scaled_ready = sem("scaled_ready")
        z_done = sem("z_done")
        z_kept = sem("z_kept")
        z_measured = sem("z_measured")
        bn_step = sem("bn_step")
        bn_inverted = sem("bn_inverted")
        bn_fold = sem("bn_fold")
        act_ready = sem("act_ready")
        y_done = sem("y_done")
        y_biased = sem("y_biased")
        y_out = sem("y_out")
        x_again = [sem(f"x_again{i}") for i in range(2)]
        out_stored = sem("out_stored")

        def block_of(b):
            return acc[:, bass.ds(b * D, D)]

        def half_block(b, k):
            return acc[:, bass.ds(b * D + k * P, P)]

        def chunk_of(c):
            return acc[:, bass.ds(c * (CH * D), CH * D)].rearrange("p (k f) -> p k f", f=D)

        def dram_chunk(dram, c):
            return dram[bass.ds(c * (CH * P), CH * P), :].rearrange("(k p) f -> p k f", p=P)

        def short_chunk(dram, sbuf):
            first = (NCH - 1) * CH * P
            cut = first + (CH - 1) * P
            return ((dram[first:cut, :].rearrange("(k p) f -> p k f", p=P), sbuf[:, 0:CH - 1, :]),
                    (dram[cut:N, :], sbuf[0:LAST, CH - 1, :]))

        def x_slot(i):
            return rows[:, i * CH * D:(i + 1) * CH * D].rearrange("p (k f) -> p k f", f=D)

        def at(table, i):
            return table[0:1, bass.ds(i, 1)]

        EDGE_DMAS = 2 * (1 + (TAIL // G > 0) + (TAIL % G > 0)) + NC_G
        CONST_DMAS = 6 + 8
        PREP_COUNT = 4
        BN = 4

        block = ctx.enter_context(nc.Block())

        @block.sync
        def _(sp):
            def load_x(c, i):
                sp.dma_start(chunk_of(c), dram_chunk(x, c)).then_inc(x_loaded[i], 16)

            load_x(0, 0)
            load_x(1, 1)
            sp.wait_ge(pool_consts, 1)
            full, q, r = (NG - 1) * GE, TAIL // G, TAIL % G
            for dram, table in ((src, src_all), (dst, dst_int)):
                sp.dma_start(table[:, 0:(NG - 1) * G].rearrange("p (g j) -> p g j", j=G),
                             dram[0:full].rearrange("(g p j) -> p g j", p=P, j=G)).then_inc(edges_loaded, 16)
                last = table[:, (NG - 1) * G:NG * G]
                if q:
                    sp.dma_start(last[0:q, :], dram[full:full + q * G].rearrange("(p j) -> p j", j=G)
                                 ).then_inc(edges_loaded, 16)
                if r:
                    sp.dma_start(last[q:q + 1, 0:r], dram[full + q * G:E].rearrange("(p j) -> p j", p=1)
                                 ).then_inc(edges_loaded, 16)
            for c in range(NC_G):
                n = min(P, NG - c * P)
                firsts = dst[c * P * GE:c * P * GE + (n - 1) * GE + 1:GE]
                sp.dma_start(group_dst_i[0:n, c:c + 1], firsts.rearrange("(p j) -> p j", j=1),
                             allow_slow_non_contiguous=True).then_inc(edges_loaded, 16)
            for i, (wa, _, _, _, wb, bb) in enumerate(layers):
                sp.dma_start(w_a[i][:, :, :], wa.rearrange("(k p) f -> p k f", p=P)).then_inc(consts_loaded, 16)
                sp.dma_start(w_b[i][:, :, :], wb.rearrange("(k p) f -> p k f", p=P)).then_inc(consts_loaded, 16)
                sp.dma_start(bias_b[i][:, :], bb.partition_broadcast(P)).then_inc(consts_loaded, 16)
            for i, v in enumerate((g0, b0, b1a, g1, bt1, b2a, g2, bt2)):
                sp.dma_start(vec[:, i, :], v.rearrange("(k p) -> p k", p=P),
                             allow_slow_non_contiguous=True).then_inc(consts_loaded, 16)

            def store_rows(t, c, done, count):
                sp.wait_ge(done, count)
                sp.dma_start(dram_chunk(tables[t], c), chunk_of(c)).then_inc(table_stored, 16)

            with sp.Fori(0, NCH // 2 - 2) as i:
                for j in range(2):
                    store_rows(0, i * 2 + j, h_ready, i * 2 + (j + 1))
                    load_x(i * 2 + (j + 2), j)
            store_rows(0, NCH - 4, h_ready, NCH - 3)
            load_x(NCH - 2, 0)
            store_rows(0, NCH - 3, h_ready, NCH - 2)
            sp.wait_ge(pool_consts, 2)
            for dram, sbuf in short_chunk(x, chunk_of(NCH - 1)):
                sp.dma_start(sbuf, dram).then_inc(x_loaded[1], 16)
            store_rows(0, NCH - 2, h_ready, NCH - 1)
            store_rows(0, NCH - 1, h_ready, NCH)

            def ring(layer):
                def group(i, j, free):
                    sp.wait_ge(slot_landed[j], i * (16 * G) + (layer * (NG // R) + 1) * 16 * G)
                    sp.sem_inc(groups_ready, 1)
                    if free:
                        first = sp.value_load(at(group_first_step, i * R + j), min_val=1, max_val=NS - 1)
                        sp.wait_ge(steps_done, first + layer * NS)
                        sp.sem_inc(groups_free, 1)

                for j in range(R):
                    group(0, j, j > 0)
                with sp.Fori(1, NG // R) as i:
                    for j in range(R):
                        group(i, j, True)
                sp.wait_ge(steps_done, (layer + 1) * NS)
                sp.sem_inc(groups_free, 1)

            sp.wait_ge(walk_ready, 1)
            sp.sem_inc(groups_free, R)
            ring(0)
            with sp.Fori(0, NCH) as c:
                store_rows(1, c, y_out, c * CH + CH)
            ring(1)

            def load_again(c, i):
                sp.dma_start(x_slot(i), dram_chunk(x, c)).then_inc(x_again[i], 16)

            load_again(0, 0)
            load_again(1, 1)
            with sp.Fori(0, NCH // 2 - 2) as i:
                for j in range(2):
                    sp.wait_ge(y_out, i * (2 * CH) + (NB + (j + 1) * CH))
                    sp.dma_start(dram_chunk(out, i * 2 + j), chunk_of(i * 2 + j)).then_inc(out_stored, 16)
                    load_again(i * 2 + (j + 2), j)
            for c in range(NCH - 4, NCH):
                sp.wait_ge(y_out, NB + (c + 1) * CH)
                if c < NCH - 1:
                    sp.dma_start(dram_chunk(out, c), chunk_of(c)).then_inc(out_stored, 16)
                if c == NCH - 4:
                    load_again(NCH - 2, 0)
                if c == NCH - 3:
                    for dram, sbuf in short_chunk(x, x_slot(1)):
                        sp.dma_start(sbuf, dram).then_inc(x_again[1], 16)
            for dram, sbuf in short_chunk(out, chunk_of(NCH - 1)):
                sp.dma_start(dram, sbuf).then_inc(out_stored, 16)
            sp.wait_ge(out_stored, 16 * (NCH + 1))

        @block.gpsimd
        def _(pool):
            pool.memset(src_all[:, (NG - 1) * G:NG * G], 0)
            pool.memset(dst_int[:, (NG - 1) * G:NG * G], -1)
            pool.memset(group_dst_i[:, :], NPAD).then_inc(pool_consts, 1)
            pool.memset(block_of(NB - 1), 0.0).then_inc(pool_consts, 1)
            pool.iota(iota_row[:, :], [[1, P]], base=0, channel_multiplier=0, allow_small_or_imprecise_dtypes=True)
            pool.iota(part_col[:, :], [[1, 1]], base=0, channel_multiplier=1, allow_small_or_imprecise_dtypes=True)
            pool.iota(block_start[:, :], [[P, NB]], base=0, channel_multiplier=0, allow_small_or_imprecise_dtypes=True)
            pool.iota(group_no[:, :], [[P, NC_G]], base=0, channel_multiplier=1, allow_small_or_imprecise_dtypes=True)
            pool.iota(walk_iota[:, :], [[1, NS]], base=0, channel_multiplier=0, allow_small_or_imprecise_dtypes=True)
            pool.memset(ones[:, :], 1.0)
            pool.memset(degree[:, :], 1.0)
            pool.memset(rows[:, :].rearrange("p (t w) -> p t w", w=RW)[:, :, D:D + 1], 1.0).then_inc(pool_consts, 1)

            def gather(layer):
                pool.wait_ge(table_stored, 16 * NCH * (layer + 1))
                with pool.Fori(0, NG // R) as i:
                    for slot in range(R):
                        pool.wait_ge(src_staged, i * R + (layer * NG + slot + 1))
                        pool.sem_inc(waits_passed, 1)
                        for t in range(slot * G, (slot + 1) * G):
                            pool.indirect_dma_start(
                                rows[:, t * RW:t * RW + D], None, tables[layer][:, :],
                                bass.IndirectOffsetOnAxis(src_stage[:, t:t + 1], 0)).then_inc(slot_landed[slot], 16)

            gather(0)
            gather(1)

        @block.tensor
        def _(pe):
            pe.sem_inc(transposed, 2)
            pe.sem_inc(z_done, 2)
            pe.sem_inc(y_done, 2)
            pe.wait_ge(pool_consts, 3)
            pe.wait_ge(setup_done, 6 + 2 * NC_G)
            for c in range(NC_G):
                mm = pe.matmul(set_ps[0:1, 0:NS], ones[:, 0:1], reached[:, c, :], start=(c == 0), stop=(c == NC_G - 1))
            mm.then_inc(setup_products, 1)
            pe.wait_ge(setup_done, 7 + 2 * NC_G)
            for c in range(NC_G):
                mm = pe.matmul(set_ps[0:1, c * P:(c + 1) * P], group_step[:, c:c + 1], ident[:, :],
                               start=(c == 0), stop=(c == NC_G - 1), skip_group_check=True)
            mm.then_inc(setup_products, 1)

            def transpose_block(n, par):
                pe.wait_ge(node_major_ready, n + 1)
                pe.wait_ge(transpose_read, n + 1)
                for k in range(KC):
                    mm = pe.transpose(tr_ps[par][:, k * P:(k + 1) * P], node_major[:, par, k * P:(k + 1) * P], ident[:, :])
                mm.then_inc(transposed, 1)

            with pe.Fori(0, NB // 2) as i:
                for j in range(2):
                    transpose_block(i * 2 + j, j)
            pe.wait_ge(bn_step, BN + 1)
            for v in range(2):
                for k in range(KC):
                    mm = pe.matmul(set_ps[:, (v * KC + k) * P:(v * KC + k + 1) * P], ones[:, :], diag[:, v, k, :],
                                   start=(v + k == 0), stop=(v + k == KC), skip_group_check=True)
            mm.then_inc(setup_products, 1)

            def walk(layer):
                width = D + 1 if layer == 0 else D
                def step(s, par):
                    group = pe.value_load(at(step_group, s), min_val=0, max_val=NG - 1)
                    slot = pe.value_load(at(step_slot, s), min_val=0, max_val=R - 1)
                    pe.wait_ge(sums_added, s + (layer * NS + 1))
                    pe.wait_ge(onehot_ready, s + (layer * NS + 1))
                    pe.wait_ge(groups_ready, group + (layer * NG + 1))
                    for t in range(G):
                        mm = pe.matmul(agg_ps[par][:, 0:width], onehot[:, par, t, :],
                                       rows[:, bass.ds(slot * (G * RW) + t * RW, width)],
                                       start=(t == 0), stop=(t == G - 1))
                    mm.then_inc(steps_done, 1)

                with pe.Fori(0, NS // 2) as i:
                    for j in range(2):
                        step(i * 2 + j, j)
                step(NS - 1, (NS - 1) % 2)

            def first_product(layer):
                def multiply(m, par):
                    pe.wait_ge(transpose_read, m + (NB + 3))
                    pe.wait_ge(z_kept, m + 1)
                    for o in range(KC):
                        for k in range(KC):
                            mm = pe.matmul(mm_ps[par][:, o * P:(o + 1) * P], w_a[layer][:, k, o * P:(o + 1) * P],
                                           feat_major[:, par, k, :], start=(o == 0 and k == 0),
                                           stop=(o == KC - 1 and k == KC - 1), skip_group_check=True)
                    mm.then_inc(z_done, 1)

                n = (layer + 1) * NB
                transpose_block(n, 0)
                with pe.Fori(0, NB // 2 - 1) as i:
                    for j in range(2):
                        transpose_block(i * 2 + (n + j + 1), 1 - j)
                        multiply(i * 2 + (layer * NB + j), j)
                transpose_block(n + NB - 1, 1)
                multiply((layer + 1) * NB - 2, 0)
                multiply((layer + 1) * NB - 1, 1)

            def second_product(layer):
                with pe.Fori(0, NB // 2) as i:
                    for j in range(2):
                        m = i * 2 + (layer * NB + j)
                        pe.wait_ge(act_ready, m + 1)
                        pe.wait_ge(y_biased, m + 1)
                        for k in range(KC):
                            mm = pe.matmul(mm_ps[j][:, 0:D], feat_major[:, j, k, :], w_b[layer][:, k, :],
                                           start=(k == 0), stop=(k == KC - 1))
                        mm.then_inc(y_done, 1)

            pe.wait_ge(consts_loaded, 16 * CONST_DMAS)
            for layer in range(2):
                walk(layer)
                first_product(layer)
                second_product(layer)

        @block.scalar
        def _(act):
            act.sem_inc(z_kept, 2)

            def stage(layer, g, slot):
                act.wait_ge(groups_free, g + (layer * NG + 1))
                act.copy(src_stage[:, slot * G:(slot + 1) * G], src_all[:, bass.ds(g * G, G)]).then_inc(src_staged, 1)

            def copy_block(b, n, par):
                act.wait_ge(transposed, n + 1)
                act.copy(node_major[:, par, :], block_of(b)).then_inc(node_major_ready, 1)

            def ln_root_of(c, j):
                act.wait_ge(ln_measured, c + 1)
                act.activation(ln_root[:, j, :], ln_var[:, j, :], ACT.Sqrt).then_inc(ln_rooted, 1)

            def normalize(i, j):
                act.wait_ge(ln_ready, i * 2 + (j + 1))
                for k in range(CH):
                    b = i * (2 * CH) + (j * CH + k)
                    ins = act.activation(block_of(b), block_of(b), ACT.Relu,
                                         bias=ln_bias[:, j, k:k + 1], scale=ln_scale[:, j, k:k + 1])
                ins.then_inc(h_ready, 1)

            ln_root_of(0, 0)
            with act.Fori(0, NCH // 2 - 1) as i:
                ln_root_of(i * 2 + 1, 1)
                normalize(i, 0)
                ln_root_of(i * 2 + 2, 0)
                normalize(i, 1)
            ln_root_of(NCH - 1, 1)
            normalize(NCH // 2 - 1, 0)
            normalize(NCH // 2 - 1, 1)

            def bn_root_of(which):
                act.wait_ge(bn_step, which * BN + (which > 0) + 2)
                act.activation(bn_root[:, :], bn_var[:, :], ACT.Sqrt).then_inc(bn_rooted, 1)

            act.wait_ge(edges_loaded, 16 * EDGE_DMAS)
            for slot in range(R):
                stage(0, slot, slot)
            act.wait_ge(h_ready, NCH)
            with act.Fori(0, NB // 2) as i:
                for j in range(2):
                    copy_block(i * 2 + j, i * 2 + j, j)
            act.wait_ge(consts_loaded, 16 * CONST_DMAS)
            bn_root_of(0)

            def dense(layer):
                bias_a = vec[:, 2 + 3 * layer, :]

                def take(b, par):
                    act.wait_ge(transposed, b + ((layer + 1) * NB + 3))
                    act.wait_ge(z_done, b + (layer * NB + 1))
                    act.copy(feat_major[:, par, :, :].rearrange("p k f -> p (k f)"), tr_ps[par][:, 0:D]
                             ).then_inc(transpose_read, 1)

                def keep(b, par):
                    act.wait_ge(z_done, b + (layer * NB + 3))
                    for k in range(KC):
                        ins = act.activation(half_block(b, k), mm_ps[par][:, k * P:(k + 1) * P], ACT.Identity,
                                             bias=bias_a[:, k:k + 1])
                    ins.then_inc(z_kept, 1)

                def ahead(b, par):
                    if layer == 1:
                        copy_block(b, b + 2 * NB, par)

                if layer == 1:
                    act.wait_ge(sums_added, 2 * NS + 2)
                ahead(0, 0)
                ahead(1, 1)
                take(0, 0)
                with act.Fori(0, NB // 2 - 1) as i:
                    for j in range(2):
                        ahead(i * 2 + (j + 2), j)
                        take(i * 2 + (j + 1), 1 - j)
                        keep(i * 2 + j, j)
                take(NB - 1, 1)
                keep(NB - 2, 0)
                keep(NB - 1, 1)
                bn_root_of(layer + 1)
                act.wait_ge(bn_step, (2 + layer) * BN + 1)
                act.wait_ge(z_kept, (layer + 1) * NB + 2)
                with act.Fori(0, NB // 2) as i:
                    for j in range(2):
                        act.wait_ge(y_done, i * 2 + (layer * NB + j + 1))
                        for k in range(KC):
                            ins = act.activation(feat_major[:, j, k, :], half_block(i * 2 + j, k), ACT.Relu,
                                                 bias=bn_shift[:, k:k + 1], scale=bn_scale[:, k:k + 1])
                        ins.then_inc(act_ready, 1)

            with act.Fori(1, NG // R) as i:
                for slot in range(R):
                    stage(0, i * R + slot, slot)
            dense(0)
            with act.Fori(0, NG // R) as i:
                for slot in range(R):
                    stage(1, i * R + slot, slot)
            dense(1)

        @block.vector
        def _(dve):
            dve.sem_inc(sums_added, 2)
            dve.sem_inc(transpose_read, 2)
            dve.sem_inc(y_biased, 2)

            def inverse_root(r, half, var, root, before, done):
                dve.reciprocal(r, root).then_inc(newton_step, 1)
                dve.wait_ge(newton_step, before + 1)
                dve.scalar_tensor_tensor(half, var, -0.5, r, ALU.mult, ALU.mult).then_inc(newton_step, 1)
                dve.wait_ge(newton_step, before + 2)
                dve.tensor_tensor(half, half, r, ALU.mult).then_inc(newton_step, 1)
                dve.wait_ge(newton_step, before + 3)
                dve.scalar_tensor_tensor(r, half, 1.5, r, ALU.add, ALU.mult).then_inc(done, 1)

            def ln_measure(i, j, c, loaded):
                dve.wait_ge(x_loaded[j], loaded)
                for k in range(CH):
                    ins = dve.bn_stats(ln_stats[:, k, :], block_of(i * (2 * CH) + (j * CH + k)))
                ins.then_inc(ln_step, 1)
                dve.wait_ge(ln_step, c * 2 + 1)
                dve.sem_inc(waits_passed, 1)
                for k in range(CH):
                    ins = dve.bn_aggr(ln_mv[:, j, k, :], ln_stats[:, k, :])
                ins.then_inc(ln_step, 1)
                dve.wait_ge(ln_step, c * 2 + 2)
                dve.tensor_scalar(ln_var[:, j, :], ln_mv[:, j, :, 1], LN_EPS, None, ALU.add).then_inc(ln_measured, 1)

            def ln_finish(j, c):
                dve.wait_ge(ln_rooted, c + 1)
                inverse_root(ln_scale[:, j, :], ln_half[:, :], ln_var[:, j, :], ln_root[:, j, :], c * 3, ln_scaled)
                dve.wait_ge(ln_scaled, c + 1)
                dve.scalar_tensor_tensor(ln_bias[:, j, :], ln_mv[:, j, :, 0], -1.0, ln_scale[:, j, :], ALU.mult, ALU.mult
                                         ).then_inc(ln_ready, 1)

            ln_measure(0, 0, 0, 16)
            with dve.Fori(0, NCH // 2 - 1) as i:
                ln_measure(i, 1, i * 2 + 1, i * 16 + 16)
                ln_finish(0, i * 2)
                ln_measure(i + 1, 0, i * 2 + 2, i * 16 + 32)
                ln_finish(1, i * 2 + 1)
            ln_measure(NCH // 2 - 1, 1, NCH - 1, (NCH // 2 + 1) * 16)
            ln_finish(0, NCH - 2)
            ln_finish(1, NCH - 1)

            done = 0

            def setup(ins):
                nonlocal done
                ins.then_inc(setup_done, 1)
                done += 1

            dve.wait_ge(pool_consts, 3)
            dve.wait_ge(edges_loaded, 16 * EDGE_DMAS)
            setup(dve.tensor_scalar(ident[:, :], iota_row[:, :], part_col[:, 0:1], None, ALU.is_equal))
            setup(dve.tensor_copy(dst_all[:, :], dst_int[:, :]))
            setup(dve.tensor_scalar(block_starts_next[:, :], block_start[:, 0:NB - 1], float(P), None, ALU.add))
            setup(dve.tensor_copy(group_dst[:, :], group_dst_i[:, :]))
            for c in range(NC_G):
                dve.wait_ge(setup_done, done)
                setup(dve.tensor_scalar(passed[:, :], block_starts_next[:, :], group_dst[:, c:c + 1], 0.0,
                                        ALU.is_le, ALU.add, accum_out=first_block[:, c:c + 1]))
            dve.wait_ge(setup_done, done)
            setup(dve.scalar_tensor_tensor(group_step[:, :], group_no[:, :], 0.0, first_block[:, :], ALU.is_gt, ALU.mult))
            dve.wait_ge(setup_done, done)
            setup(dve.tensor_tensor(group_step[:, :], group_step[:, :], group_no[:, :], ALU.add))
            dve.wait_ge(setup_done, done)
            for c in range(NC_G):
                setup(dve.tensor_scalar(reached[:, c, :], walk_iota[:, :], group_step[:, c:c + 1], None, ALU.is_ge))
            dve.wait_ge(setup_products, 1)
            setup(dve.tensor_scalar(step_group[:, :], set_ps[0:1, 0:NS], -1.0, None, ALU.add))
            dve.wait_ge(setup_products, 2)
            dve.tensor_copy(group_first_step[:, :], set_ps[0:1, 0:NC_G * P])
            dve.wait_ge(setup_done, done)
            dve.tensor_scalar(step_slot[:, :], step_group[:, :], R - 1, None, ALU.bitwise_and).then_inc(walk_ready, 1)

            def measure(half, b, width):
                for k in range(KC):
                    ins = dve.bn_stats(bn_stats[:, k, bass.ds(b * 6, 6)], half(k)[:, 0:width])
                return ins

            def measure_h(b, par, width):
                dve.wait_ge(transposed, b + 3)
                measure(lambda k: tr_ps[par][:, k * P:(k + 1) * P], b, width).then_inc(transpose_read, 1)

            with dve.Fori(0, NB // 2 - 1) as i:
                for j in range(2):
                    measure_h(i * 2 + j, j, P)
            measure_h(NB - 2, 0, P)
            measure_h(NB - 1, 1, LAST)

            def scale_and_shift(which, gamma, beta):
                for k in range(KC):
                    ins = dve.bn_aggr(bn_mv[:, k, :], bn_stats[:, k, :])
                ins.then_inc(bn_step, 1)
                base = which * BN + (which > 0)
                dve.wait_ge(bn_step, base + 1)
                dve.tensor_scalar(bn_var[:, :], bn_mv[:, :, 1], BN_EPS, None, ALU.add).then_inc(bn_step, 1)
                dve.wait_ge(bn_rooted, which + 1)
                inverse_root(bn_rstd[:, :], bn_half[:, :], bn_var[:, :], bn_root[:, :], 3 * (NCH + which), bn_inverted)
                dve.wait_ge(bn_inverted, which + 1)
                dve.tensor_tensor(bn_scale[:, :], bn_rstd[:, :], gamma, ALU.mult).then_inc(bn_step, 1)
                dve.wait_ge(bn_step, base + 3)
                dve.scalar_tensor_tensor(bn_shift[:, :], bn_mv[:, :, 0], -1.0, bn_scale[:, :], ALU.mult, ALU.mult
                                         ).then_inc(bn_fold, 1)
                dve.wait_ge(bn_fold, which + 1)
                dve.tensor_tensor(bn_shift[:, :], bn_shift[:, :], beta, ALU.add).then_inc(bn_step, 1)
                dve.wait_ge(bn_step, base + 4)

            dve.wait_ge(consts_loaded, 16 * CONST_DMAS)
            dve.wait_ge(transpose_read, NB + 2)
            scale_and_shift(0, vec[:, 0, :], vec[:, 1, :])
            for v, column in enumerate((bn_scale, bn_shift)):
                for k in range(KC):
                    ins = dve.tensor_scalar(diag[:, v, k, :], ident[:, :], column[:, k:k + 1], None, ALU.mult)
            ins.then_inc(bn_step, 1)
            dve.wait_ge(setup_products, 3)
            dve.tensor_copy(affine_rows[:, :, :].rearrange("p v f -> p (v f)"), set_ps[:, :]).then_inc(setup_done, 1)
            done += 1

            def walk(layer):
                def place(s, par):
                    group = dve.value_load(at(step_group, s), min_val=0, max_val=NG - 1)
                    b = nc.s_assert_within(s - group, 0, NB - 1, skip_runtime_bounds_check_because="the walk ends at the last block")
                    dve.scalar_tensor_tensor(
                        onehot[:, par, :, :],
                        dst_all[:, bass.ds(group * G, G)].unsqueeze(2).to_broadcast([P, G, P]),
                        block_start[:, bass.ds(b, 1)],
                        iota_row[:, :].unsqueeze(1).to_broadcast([P, G, P]),
                        ALU.subtract, ALU.is_equal).then_inc(onehot_ready, 1)

                def add(s, par):
                    group = dve.value_load(at(step_group, s), min_val=0, max_val=NG - 1)
                    b = nc.s_assert_within(s - group, 0, NB - 1, skip_runtime_bounds_check_because="the walk ends at the last block")
                    dve.wait_ge(steps_done, s + (layer * NS + 1))
                    dve.wait_ge(sums_added, s + (layer * NS + 2))
                    if layer == 0:
                        dve.tensor_tensor(degree[:, bass.ds(b, 1)], degree[:, bass.ds(b, 1)],
                                          agg_ps[par][:, D:D + 1], ALU.add)
                    dve.tensor_tensor(block_of(b), block_of(b), agg_ps[par][:, 0:D], ALU.add).then_inc(sums_added, 1)

                place(0, 0)
                with dve.Fori(0, NS // 2) as i:
                    for j in range(2):
                        place(i * 2 + (j + 1), 1 - j)
                        add(i * 2 + j, j)
                add(NS - 1, (NS - 1) % 2)

            def dense(layer):
                first = layer * NB

                def affine(b, par):
                    dve.tensor_tensor(scaled[:, par, :], block_of(b), affine_rows[:, 0, :], ALU.mult
                                      ).then_inc(scaled_ready, 1)
                    dve.wait_ge(transposed, b + (NB + 1))
                    dve.wait_ge(scaled_ready, b + 1)
                    dve.scalar_tensor_tensor(node_major[:, par, :], affine_rows[:, 1, :], degree[:, bass.ds(b, 1)],
                                             scaled[:, par, :], ALU.mult, ALU.add).then_inc(node_major_ready, 1)

                def measure_z(b, width):
                    dve.wait_ge(z_kept, b + (first + 3))
                    measure(lambda k: half_block(b, k), b, width).then_inc(z_measured, 1)

                dve.wait_ge(sums_added, (layer + 1) * NS + 2)
                if layer == 0:
                    dve.wait_ge(setup_done, done)
                    affine(0, 0)
                with dve.Fori(0, NB // 2 - 1) as i:
                    for j in range(2):
                        if layer == 0:
                            affine(i * 2 + (j + 1), 1 - j)
                        measure_z(i * 2 + j, P)
                if layer == 0:
                    affine(NB - 1, 1)
                measure_z(NB - 2, P)
                measure_z(NB - 1, LAST)
                dve.wait_ge(z_measured, first + NB)
                scale_and_shift(layer + 1, vec[:, 3 + 3 * layer, :], vec[:, 4 + 3 * layer, :])

                def finish(i, x_odd):
                    for u in range(2 * CH):
                        par, b = u % 2, i * (2 * CH) + u
                        if layer == 1 and u == 0:
                            dve.wait_ge(x_again[0], i * 16 + 16)
                        if layer == 1 and u == CH:
                            dve.wait_ge(x_again[1], x_odd)
                        dve.wait_ge(y_done, b + (first + 3))
                        dve.tensor_tensor(pre_relu[:, par, :], mm_ps[par][:, 0:D], bias_b[layer][:, :], ALU.add
                                          ).then_inc(y_biased, 1)
                        dve.wait_ge(y_biased, b + (first + 3))
                        if layer == 0:
                            dve.tensor_scalar(block_of(b), pre_relu[:, par, :], 0.0, None, ALU.max).then_inc(y_out, 1)
                        else:
                            dve.scalar_tensor_tensor(block_of(b), pre_relu[:, par, :], 0.0, x_slot(u // CH)[:, u % CH, :],
                                                     ALU.max, ALU.add).then_inc(y_out, 1)

                with dve.Fori(0, NCH // 2 - 1) as i:
                    finish(i, i * 16 + 16)
                finish(NCH // 2 - 1, (NCH // 2 + 1) * 16)

            for layer in range(2):
                walk(layer)
                dense(layer)


_INS = ["x", "src", "dst"] + [f"L0_gnn_{n}" for n in
                              ("g0", "b0", "W1a", "b1a", "g1", "bt1", "W1b", "b1b", "W2a", "b2a", "g2", "bt2", "W2b", "b2b")]


def kernel(**inputs):
    import numpy as np
    import concourse.bacc as bacc
    from concourse.bass_utils import run_bass_kernel_spmd

    nc = bacc.Bacc("TRN2", target_bir_lowering=False, num_devices=1)
    arrays, aps = {}, []
    for name in _INS:
        a = np.ascontiguousarray(inputs[name])
        arrays[f"in_{name}"] = a
        aps.append(nc.dram_tensor(f"in_{name}", a.shape, mybir.dt.from_np(a.dtype), kind="ExternalInput").ap())
    out = nc.dram_tensor("out_0", (N, D), F32, kind="ExternalOutput").ap()
    build(nc, *aps, out)
    r = run_bass_kernel_spmd(nc, [arrays], core_ids=[0])
    return r.results[0]["out_0"]
```

```python
from contextlib import ExitStack

import concourse.bass as bass
from concourse import mybir

P = 128
N = 12500
D = 256
E = 212500
KC = D // P
LN_EPS = 1e-5
BN_EPS = 1e-5

NB = (N + P - 1) // P
NPAD = NB * P
LAST = N - (NB - 1) * P
CH = 7
NCH = NB // CH
LB = NCH // 2
EARLY = NB // CH
G = 8
GE = G * P
NG = (E + GE - 1) // GE
TAIL = E - (NG - 1) * GE
NS = NG + NB - 1
R = 4
RW = 272
NC_G = (NG + P - 1) // P

F32 = mybir.dt.float32
I32 = mybir.dt.int32
ALU = mybir.AluOpType
ACT = mybir.ActivationFunctionType


def build(nc, x, src, dst, g0, b0, W1a, b1a, g1, bt1, W1b, b1b, W2a, b2a, g2, bt2, W2b, b2b, out):
    tables = [nc.dram_tensor(f"node_rows_{i}", (NPAD, D), F32, kind="Internal").ap() for i in range(2)]
    layers = [(W1a, b1a, g1, bt1, W1b, b1b), (W2a, b2a, g2, bt2, W2b, b2b)]

    ctx = ExitStack()
    with ctx:
        def sb(name, shape, dt=F32):
            return ctx.enter_context(nc.sbuf_tensor(name, shape, dt))

        def pb(name, shape):
            return ctx.enter_context(nc.psum_tensor(name, shape, F32))

        def sem(name):
            return ctx.enter_context(nc.semaphore(name))

        acc = sb("acc", [P, (NB + 1) * D])
        degree = sb("degree", [P, NB])
        rows = sb("rows", [P, R * G * RW])
        dst_int = sb("dst_int", [P, NG * G], I32)
        dst_all = sb("dst_all", [P, NG * G])
        src_stage = sb("src_stage", [P, R * G], I32)
        onehot = sb("onehot", [P, 2, G, P])
        iota_row = sb("iota_row", [P, P])
        part_col = sb("part_col", [P, 1])
        ident = sb("ident", [P, P])
        ones = sb("ones", [P, P])
        block_start = sb("block_start", [P, NB])
        block_starts_next = sb("block_starts_next", [P, NB - 1])
        walk_iota = sb("walk_iota", [P, NS])
        group_no = sb("group_no", [P, NC_G])
        group_dst_i = sb("group_dst_i", [P, NC_G], I32)
        group_dst = sb("group_dst", [P, NC_G])
        passed = sb("passed", [P, NB - 1])
        first_block = sb("first_block", [P, NC_G])
        group_step = sb("group_step", [P, NC_G])
        reached = sb("reached", [P, NC_G, NS])
        step_group = sb("step_group", [1, NS], I32)
        step_block = sb("step_block", [1, NS], I32)
        step_slot = sb("step_slot", [1, NS], I32)
        step_ends = sb("step_ends", [1, NS], I32)
        group_first_step = sb("group_first_step", [1, NC_G * P], I32)
        w_a = [sb(f"w_a{i}", [P, KC, D]) for i in range(2)]
        w_b = [sb(f"w_b{i}", [P, KC, D]) for i in range(2)]
        vec = sb("vec", [P, 8, KC])
        bias_b = [sb(f"bias_b{i}", [P, D]) for i in range(2)]
        ln_stats = sb("ln_stats", [P, CH, 6])
        ln_mv = sb("ln_mv", [P, LB, CH, 2])
        ln_var = sb("ln_var", [P, LB, CH])
        ln_root = sb("ln_root", [P, LB, CH])
        ln_half = sb("ln_half", [P, CH])
        ln_scale = sb("ln_scale", [P, LB, CH])
        ln_bias = sb("ln_bias", [P, LB, CH])
        bn_stats = sb("bn_stats", [P, KC, (NB + 1) * 6])
        bn_mv = sb("bn_mv", [P, KC, 2])
        bn_rstd = sb("bn_rstd", [P, KC])
        bn_scale = sb("bn_scale", [P, KC])
        bn_shift = sb("bn_shift", [P, KC])
        bn_var = sb("bn_var", [P, KC])
        bn_root = sb("bn_root", [P, KC])
        bn_half = sb("bn_half", [P, KC])
        diag = sb("diag", [P, 2, KC, P])
        affine_rows = sb("affine_rows", [P, 2, D])
        scaled = sb("scaled", [P, D])
        node_major = sb("node_major", [P, CH, D])
        feat_major = sb("feat_major", [P, CH, KC, P])
        pre_relu = sb("pre_relu", [P, 2, D])

        agg_ps = [pb(f"agg_ps{i}", [P, 512]) for i in range(2)]
        tr_ps = [pb(f"tr_ps{i}", [P, 512]) for i in range(2)]
        mm_ps = [pb(f"mm_ps{i}", [P, 512]) for i in range(2)]
        set_ps = pb("set_ps", [P, 512])

        x_loaded = [sem(f"x_loaded{i}") for i in range(LB)]
        edges_loaded = sem("edges_loaded")
        consts_loaded = sem("consts_loaded")
        pool_consts = sem("pool_consts")
        setup_done = sem("setup_done")
        setup_products = sem("setup_products")
        walk_ready = sem("walk_ready")
        ln_step = sem("ln_step")
        waits_passed = sem("waits_passed")
        newton_step = sem("newton_step")
        ln_measured = sem("ln_measured")
        ln_scaled = sem("ln_scaled")
        ln_rooted = sem("ln_rooted")
        bn_rooted = sem("bn_rooted")
        ln_ready = sem("ln_ready")
        h_ready = sem("h_ready")
        table_stored = sem("table_stored")
        src_staged = [sem(f"src_staged{i}") for i in range(R)]
        slot_landed = [sem(f"slot_landed{i}") for i in range(R)]
        groups_ready = sem("groups_ready")
        onehot_ready = sem("onehot_ready")
        steps_done = sem("steps_done")
        sums_added = sem("sums_added")
        node_major_ready = sem("node_major_ready")
        transposed = sem("transposed")
        transpose_read = sem("transpose_read")
        sum_scaled = sem("sum_scaled")
        sum_ready = sem("sum_ready")
        sum_transposed = sem("sum_transposed")
        sum_taken = sem("sum_taken")
        z_done = sem("z_done")
        z_kept = sem("z_kept")
        z_measured = sem("z_measured")
        bn_step = sem("bn_step")
        bn_inverted = sem("bn_inverted")
        bn_fold = sem("bn_fold")
        act_ready = sem("act_ready")
        y_done = sem("y_done")
        y_biased = sem("y_biased")
        y_out = sem("y_out")
        x_again = [sem(f"x_again{i}") for i in range(2)]
        out_stored = sem("out_stored")

        def block_of(b):
            return acc[:, bass.ds(b * D + D, D)]

        def half_block(b, k):
            return acc[:, bass.ds(b * D + (D + k * P), P)]

        def chunk_of(c):
            return acc[:, bass.ds(c * (CH * D) + D, CH * D)].rearrange("p (k f) -> p k f", f=D)

        def dram_chunk(dram, c):
            return dram[bass.ds(c * (CH * P), CH * P), :].rearrange("(k p) f -> p k f", p=P)

        def short_chunk(dram, sbuf):
            first = (NCH - 1) * CH * P
            cut = first + (CH - 1) * P
            return ((dram[first:cut, :].rearrange("(k p) f -> p k f", p=P), sbuf[:, 0:CH - 1, :]),
                    (dram[cut:N, :], sbuf[0:LAST, CH - 1, :]))

        def x_slot(i):
            return rows[:, i * CH * D:(i + 1) * CH * D].rearrange("p (k f) -> p k f", f=D)

        def at(table, i):
            return table[0:1, bass.ds(i, 1)]

        TAIL_DMAS = (TAIL // G > 0) + (TAIL % G > 0)
        EDGE_DMAS = 1 + TAIL_DMAS + NC_G
        CONST_DMAS = 6 + 8
        BN = 4

        block = ctx.enter_context(nc.Block())

        @block.sync
        def _(sp):
            for c in range(LB):
                sp.dma_start(chunk_of(c), dram_chunk(x, c)).then_inc(x_loaded[c], 16)
            sp.wait_ge(pool_consts, 1)
            full, q, r = (NG - 1) * GE, TAIL // G, TAIL % G

            def load_tail(dram, last, done):
                if q:
                    sp.dma_start(last[0:q, :], dram[full:full + q * G].rearrange("(p j) -> p j", j=G)).then_inc(done, 16)
                if r:
                    sp.dma_start(last[q:q + 1, 0:r], dram[full + q * G:E].rearrange("(p j) -> p j", p=1)).then_inc(done, 16)

            for c in range(LB - 1):
                sp.wait_ge(x_loaded[c], 16)
                sp.dma_start(chunk_of(LB + c), dram_chunk(x, LB + c)).then_inc(x_loaded[c], 16)
            sp.wait_ge(x_loaded[LB - 1], 16)
            for dram, sbuf in short_chunk(x, chunk_of(NCH - 1)):
                sp.dma_start(sbuf, dram).then_inc(x_loaded[LB - 1], 16)
            sp.dma_start(dst_int[:, 0:(NG - 1) * G].rearrange("p (g j) -> p g j", j=G),
                         dst[0:full].rearrange("(g p j) -> p g j", p=P, j=G)).then_inc(edges_loaded, 16)
            load_tail(dst, dst_int[:, (NG - 1) * G:NG * G], edges_loaded)
            for c in range(NC_G):
                n = min(P, NG - c * P)
                firsts = dst[c * P * GE:c * P * GE + (n - 1) * GE + 1:GE]
                sp.dma_start(group_dst_i[0:n, c:c + 1], firsts.rearrange("(p j) -> p j", j=1),
                             allow_slow_non_contiguous=True).then_inc(edges_loaded, 16)
            for i, (wa, _, _, _, wb, bb) in enumerate(layers):
                sp.dma_start(w_a[i][:, :, :], wa.rearrange("(k p) f -> p k f", p=P)).then_inc(consts_loaded, 16)
                sp.dma_start(w_b[i][:, :, :], wb.rearrange("(k p) f -> p k f", p=P)).then_inc(consts_loaded, 16)
                sp.dma_start(bias_b[i][:, :], bb.partition_broadcast(P)).then_inc(consts_loaded, 16)
            for i, v in enumerate((g0, b0, b1a, g1, bt1, b2a, g2, bt2)):
                sp.dma_start(vec[:, i, :], v.rearrange("(k p) -> p k", p=P),
                             allow_slow_non_contiguous=True).then_inc(consts_loaded, 16)

            def stage(g, slot):
                sp.dma_start(src_stage[:, slot * G:(slot + 1) * G],
                             src[bass.ds(g * GE, GE)].rearrange("(p j) -> p j", j=G)).then_inc(src_staged[slot], 16)

            def store_rows(t, c, done, count):
                sp.wait_ge(done, count)
                sp.dma_start(dram_chunk(tables[t], c), chunk_of(c)).then_inc(table_stored, 16)

            for slot in range(R):
                stage(slot, slot)
            with sp.Fori(0, NCH) as c:
                store_rows(0, c, h_ready, c + 1)

            def ring(layer):
                def group(i, j, refill):
                    sp.wait_ge(slot_landed[j], i * (16 * G) + (layer * (NG // R) + 1) * 16 * G)
                    sp.sem_inc(groups_ready, 1)
                    if refill:
                        first = sp.value_load(at(group_first_step, i * R + j), min_val=1, max_val=NS - 1)
                        sp.wait_ge(steps_done, first + layer * NS)
                        refill(i, j)

                def usual(i, j):
                    stage(i * R + (j - 1 + R), (j - 1) % R)

                def tail(i, j):
                    load_tail(src, src_stage[:, (R - 1) * G:R * G], src_staged[R - 1])

                for j in range(R):
                    group(0, j, usual if j else None)
                with sp.Fori(1, NG // R - 1) as i:
                    for j in range(R):
                        group(i, j, usual)
                group(NG // R - 1, 0, tail)
                for j in range(1, R):
                    group(NG // R - 1, j, None)

            sp.wait_ge(walk_ready, 1)
            ring(0)
            sp.wait_ge(steps_done, NS)
            for slot in range(R):
                stage(slot, slot)
            with sp.Fori(0, NCH) as c:
                store_rows(1, c, y_out, c * CH + CH)
            ring(1)
            sp.wait_ge(steps_done, 2 * NS)

            def load_again(c, i):
                sp.dma_start(x_slot(i), dram_chunk(x, c)).then_inc(x_again[i], 16)

            load_again(0, 0)
            load_again(1, 1)
            with sp.Fori(0, NCH // 2 - 2) as i:
                for j in range(2):
                    sp.wait_ge(y_out, i * (2 * CH) + (NB + (j + 1) * CH))
                    sp.dma_start(dram_chunk(out, i * 2 + j), chunk_of(i * 2 + j)).then_inc(out_stored, 16)
                    load_again(i * 2 + (j + 2), j)
            for c in range(NCH - 4, NCH):
                sp.wait_ge(y_out, NB + (c + 1) * CH)
                if c < NCH - 1:
                    sp.dma_start(dram_chunk(out, c), chunk_of(c)).then_inc(out_stored, 16)
                if c == NCH - 4:
                    load_again(NCH - 2, 0)
                if c == NCH - 3:
                    for dram, sbuf in short_chunk(x, x_slot(1)):
                        sp.dma_start(sbuf, dram).then_inc(x_again[1], 16)
            for dram, sbuf in short_chunk(out, chunk_of(NCH - 1)):
                sp.dma_start(dram, sbuf).then_inc(out_stored, 16)
            sp.wait_ge(out_stored, 16 * (NCH + 1))

        @block.gpsimd
        def _(pool):
            pool.memset(dst_int[:, (NG - 1) * G:NG * G], -1)
            pool.memset(group_dst_i[:, :], NPAD)
            pool.memset(block_of(-1), 0.0)
            pool.memset(block_of(NB - 1), 0.0).then_inc(pool_consts, 1)
            pool.iota(iota_row[:, :], [[1, P]], base=0, channel_multiplier=0, allow_small_or_imprecise_dtypes=True)
            pool.iota(part_col[:, :], [[1, 1]], base=0, channel_multiplier=1, allow_small_or_imprecise_dtypes=True)
            pool.iota(block_start[:, :], [[P, NB]], base=0, channel_multiplier=0, allow_small_or_imprecise_dtypes=True)
            pool.iota(group_no[:, :], [[P, NC_G]], base=0, channel_multiplier=1, allow_small_or_imprecise_dtypes=True)
            pool.iota(walk_iota[:, :], [[1, NS]], base=0, channel_multiplier=0, allow_small_or_imprecise_dtypes=True)
            pool.memset(ones[:, :], 1.0)
            pool.memset(degree[:, :], 1.0)
            pool.memset(rows[:, :].rearrange("p (t w) -> p t w", w=RW)[:, :, D:D + 1], 1.0).then_inc(pool_consts, 1)

            def gather(layer):
                pool.wait_ge(table_stored, 16 * NCH * (layer + 1))
                def slot_of(slot, staged):
                    pool.wait_ge(src_staged[slot], staged)
                    pool.sem_inc(waits_passed, 1)
                    for t in range(slot * G, (slot + 1) * G):
                        pool.indirect_dma_start(
                            rows[:, t * RW:t * RW + D], None, tables[layer][:, :],
                            bass.IndirectOffsetOnAxis(src_stage[:, t:t + 1], 0)).then_inc(slot_landed[slot], 16)

                before = [layer * (NG // R + (TAIL_DMAS - 1 if slot == R - 1 else 0)) * 16 for slot in range(R)]
                with pool.Fori(0, NG // R - 1) as i:
                    for slot in range(R):
                        slot_of(slot, i * 16 + (before[slot] + 16))
                for slot in range(R):
                    slot_of(slot, before[slot] + (NG // R - 1 + (TAIL_DMAS if slot == R - 1 else 1)) * 16)

            gather(0)
            gather(1)

        @block.tensor
        def _(pe):
            pe.sem_inc(transposed, CH)
            pe.sem_inc(y_done, CH)
            pe.wait_ge(pool_consts, 2)
            pe.wait_ge(setup_done, 6 + 2 * NC_G)
            for c in range(NC_G):
                mm = pe.matmul(set_ps[0:1, 0:NS], ones[:, 0:1], reached[:, c, :], start=(c == 0), stop=(c == NC_G - 1))
            mm.then_inc(setup_products, 1)
            pe.wait_ge(setup_done, 7 + 2 * NC_G)
            for c in range(NC_G):
                mm = pe.matmul(set_ps[0:1, c * P:(c + 1) * P], group_step[:, c:c + 1], ident[:, :],
                               start=(c == 0), stop=(c == NC_G - 1), skip_group_check=True)
            mm.then_inc(setup_products, 1)

            def transpose_block(n, u):
                pe.wait_ge(node_major_ready, n + 1)
                pe.wait_ge(transpose_read, n + 1)
                for k in range(KC):
                    mm = pe.transpose(tr_ps[u % 2][:, k * P:(k + 1) * P], node_major[:, u % CH, k * P:(k + 1) * P],
                                      ident[:, :])
                mm.then_inc(transposed, 1)

            def affine_to_rows():
                pe.wait_ge(bn_step, BN + 1)
                for v in range(2):
                    for k in range(KC):
                        mm = pe.matmul(set_ps[:, (v * KC + k) * P:(v * KC + k + 1) * P], ones[:, :], diag[:, v, k, :],
                                       start=(v + k == 0), stop=(v + k == KC), skip_group_check=True)
                mm.then_inc(setup_products, 1)

            def walk(layer):
                width = D + 1 if layer == 0 else D
                pe.wait_ge(walk_ready, 1)

                def step(s, par, between=None):
                    slot = pe.value_load(at(step_slot, s), min_val=0, max_val=R - 1)
                    group = pe.value_load(at(step_group, s), min_val=0, max_val=NG - 1)
                    pe.wait_ge(sums_added, s + (layer * NS + 1))
                    pe.wait_ge(onehot_ready, s + (layer * NS + 1))
                    pe.wait_ge(groups_ready, group + (layer * NG + 1))
                    for t in range(G):
                        mm = pe.matmul(agg_ps[par][:, 0:width], onehot[:, par, t, :],
                                       rows[:, bass.ds(slot * (G * RW) + t * RW, width)],
                                       start=(t == 0), stop=(t == G - 1))
                        if t == G - 1:
                            mm.then_inc(steps_done, 1)
                        elif between:
                            between(t)

                def end_block(s):
                    ended = pe.value_load(at(step_ends, s - 1), min_val=0, max_val=1)
                    with pe.If(ended == 1):
                        first_product(pe.value_load(at(step_block, s), min_val=1, max_val=NB - 1))

                def first_product(block_done):
                    pe.wait_ge(sum_ready, block_done + layer * NB)
                    for k in range(KC):
                        mm = pe.transpose(tr_ps[0][:, k * P:(k + 1) * P], node_major[:, 0, k * P:(k + 1) * P], ident[:, :])
                    mm.then_inc(sum_transposed, 1)
                    pe.wait_ge(sum_taken, block_done + layer * NB)
                    for o in range(KC):
                        for k in range(KC):
                            mm = pe.matmul(mm_ps[0][:, o * P:(o + 1) * P], w_a[layer][:, k, o * P:(o + 1) * P],
                                           feat_major[:, 0, k, :], start=(o == 0 and k == 0),
                                           stop=(o == KC - 1 and k == KC - 1), skip_group_check=True)
                    mm.then_inc(z_done, 1)

                if layer == 0:
                    with pe.Fori(0, EARLY // 2) as i:
                        for j in range(2):
                            step(i * 2 + j, j, lambda u: transpose_block(i * (2 * CH) + (j * CH + u), j * CH + u))
                    affine_to_rows()
                    step(EARLY, EARLY % 2)
                    end_block(1)
                    with pe.Fori(0, EARLY // 2) as i:
                        for j in range(2):
                            step(i * 2 + (EARLY + 1 + j), (EARLY + 1 + j) % 2)
                            for u in range(2):
                                end_block(i * 4 + (2 + 2 * j + u))
                else:
                    step(0, 0)
                    with pe.Fori(0, EARLY) as i:
                        for j in range(2):
                            step(i * 2 + (j + 1), 1 - j)
                            end_block(i * 2 + (j + 1))
                with pe.Fori(EARLY, NS // 2) as i:
                    for j in range(2):
                        step(i * 2 + (j + 1), 1 - j)
                        end_block(i * 2 + (j + 1))
                first_product(NB)

            def second_product(layer):
                with pe.Fori(0, NB // (2 * CH)) as i:
                    for u in range(2 * CH):
                        par, m = u % 2, i * (2 * CH) + (layer * NB + u)
                        pe.wait_ge(act_ready, m + 1)
                        pe.wait_ge(y_biased, m + 1)
                        for k in range(KC):
                            mm = pe.matmul(mm_ps[par][:, 0:D], feat_major[:, u % CH, k, :], w_b[layer][:, k, :],
                                           start=(k == 0), stop=(k == KC - 1))
                        mm.then_inc(y_done, 1)

            pe.wait_ge(consts_loaded, 16 * CONST_DMAS)
            for layer in range(2):
                walk(layer)
                second_product(layer)

        @block.scalar
        def _(act):
            act.sem_inc(z_kept, 1)

            def copy_block(b, u):
                act.wait_ge(transposed, b + 1)
                act.copy(node_major[:, u % CH, :], block_of(b)).then_inc(node_major_ready, 1)

            def ln_root_of(i, k):
                act.wait_ge(ln_measured, i * LB + (k + 1))
                act.activation(ln_root[:, k, :], ln_var[:, k, :], ACT.Sqrt).then_inc(ln_rooted, 1)

            def normalize(i, k):
                act.wait_ge(ln_ready, i * LB + (k + 1))
                for u in range(CH):
                    b = i * (LB * CH) + (k * CH + u)
                    ins = act.activation(block_of(b), block_of(b), ACT.Relu,
                                         bias=ln_bias[:, k, u:u + 1], scale=ln_scale[:, k, u:u + 1])
                ins.then_inc(h_ready, 1)

            with act.Fori(0, 2) as i:
                for k in range(LB):
                    ln_root_of(i, k)
                    if k:
                        normalize(i, k - 1)
                normalize(i, LB - 1)

            def bn_root_of(which):
                act.wait_ge(bn_step, which * BN + (which > 0) + 2)
                act.activation(bn_root[:, :], bn_var[:, :], ACT.Sqrt).then_inc(bn_rooted, 1)

            act.wait_ge(h_ready, NCH)
            with act.Fori(0, NCH) as c:
                for u in range(CH):
                    copy_block(c * CH + u, u)
            act.wait_ge(consts_loaded, 16 * CONST_DMAS)
            bn_root_of(0)

            def dense(layer):
                bias_a = vec[:, 2 + 3 * layer, :]

                with act.Fori(0, NB) as b:
                    act.wait_ge(sum_transposed, b + (layer * NB + 1))
                    act.copy(feat_major[:, 0, :, :].rearrange("p k f -> p (k f)"), tr_ps[0][:, 0:D]).then_inc(sum_taken, 1)
                    act.wait_ge(z_done, b + (layer * NB + 1))
                    for k in range(KC):
                        ins = act.activation(half_block(b, k), mm_ps[0][:, k * P:(k + 1) * P], ACT.Identity,
                                             bias=bias_a[:, k:k + 1])
                    ins.then_inc(z_kept, 1)
                bn_root_of(layer + 1)
                act.wait_ge(bn_step, (2 + layer) * BN + 1)
                act.wait_ge(z_kept, (layer + 1) * NB + 1)
                with act.Fori(0, NB // (2 * CH)) as i:
                    for u in range(2 * CH):
                        b = i * (2 * CH) + u
                        act.wait_ge(y_done, b + (layer * NB + 1))
                        for k in range(KC):
                            ins = act.activation(feat_major[:, u % CH, k, :], half_block(b, k), ACT.Relu,
                                                 bias=bn_shift[:, k:k + 1], scale=bn_scale[:, k:k + 1])
                        ins.then_inc(act_ready, 1)

            dense(0)
            dense(1)

        @block.vector
        def _(dve):
            dve.sem_inc(sums_added, 2)
            dve.sem_inc(transpose_read, 2)
            dve.sem_inc(y_biased, 2)

            def inverse_root(r, half, var, root, before, done):
                dve.reciprocal(r, root).then_inc(newton_step, 1)
                dve.wait_ge(newton_step, before + 1)
                dve.scalar_tensor_tensor(half, var, -0.5, r, ALU.mult, ALU.mult).then_inc(newton_step, 1)
                dve.wait_ge(newton_step, before + 2)
                dve.tensor_tensor(half, half, r, ALU.mult).then_inc(newton_step, 1)
                dve.wait_ge(newton_step, before + 3)
                dve.scalar_tensor_tensor(r, half, 1.5, r, ALU.add, ALU.mult).then_inc(done, 1)

            def ln_measure(i, k):
                dve.wait_ge(x_loaded[k], i * (32 if k == LB - 1 else 16) + 16)
                for u in range(CH):
                    ins = dve.bn_stats(ln_stats[:, u, :], block_of(i * (LB * CH) + (k * CH + u)))
                ins.then_inc(ln_step, 1)
                dve.wait_ge(ln_step, i * (2 * LB) + (2 * k + 1))
                dve.sem_inc(waits_passed, 1)
                for u in range(CH):
                    ins = dve.bn_aggr(ln_mv[:, k, u, :], ln_stats[:, u, :])
                ins.then_inc(ln_step, 1)
                dve.wait_ge(ln_step, i * (2 * LB) + (2 * k + 2))
                dve.tensor_scalar(ln_var[:, k, :], ln_mv[:, k, :, 1], LN_EPS, None, ALU.add).then_inc(ln_measured, 1)

            def ln_finish(i, k):
                dve.wait_ge(ln_rooted, i * LB + (k + 1))
                inverse_root(ln_scale[:, k, :], ln_half[:, :], ln_var[:, k, :], ln_root[:, k, :],
                             i * (3 * LB) + 3 * k, ln_scaled)
                dve.wait_ge(ln_scaled, i * LB + (k + 1))
                dve.scalar_tensor_tensor(ln_bias[:, k, :], ln_mv[:, k, :, 0], -1.0, ln_scale[:, k, :], ALU.mult, ALU.mult
                                         ).then_inc(ln_ready, 1)

            with dve.Fori(0, 2) as i:
                for k in range(LB):
                    ln_measure(i, k)
                    if k:
                        ln_finish(i, k - 1)
                ln_finish(i, LB - 1)

            done = 0

            def setup(ins):
                nonlocal done
                ins.then_inc(setup_done, 1)
                done += 1

            dve.wait_ge(pool_consts, 2)
            dve.wait_ge(edges_loaded, 16 * EDGE_DMAS)
            setup(dve.tensor_scalar(ident[:, :], iota_row[:, :], part_col[:, 0:1], None, ALU.is_equal))
            setup(dve.tensor_copy(dst_all[:, :], dst_int[:, :]))
            setup(dve.tensor_scalar(block_starts_next[:, :], block_start[:, 0:NB - 1], float(P), None, ALU.add))
            setup(dve.tensor_copy(group_dst[:, :], group_dst_i[:, :]))
            for c in range(NC_G):
                dve.wait_ge(setup_done, done)
                setup(dve.tensor_scalar(passed[:, :], block_starts_next[:, :], group_dst[:, c:c + 1], 0.0,
                                        ALU.is_le, ALU.add, accum_out=first_block[:, c:c + 1]))
            dve.wait_ge(setup_done, done)
            setup(dve.scalar_tensor_tensor(group_step[:, :], group_no[:, :], 0.0, first_block[:, :], ALU.is_gt, ALU.mult))
            dve.wait_ge(setup_done, done)
            setup(dve.tensor_tensor(group_step[:, :], group_step[:, :], group_no[:, :], ALU.add))
            dve.wait_ge(setup_done, done)
            for c in range(NC_G):
                setup(dve.tensor_scalar(reached[:, c, :], walk_iota[:, :], group_step[:, c:c + 1], None, ALU.is_ge))
            dve.wait_ge(setup_products, 1)
            setup(dve.tensor_scalar(step_group[:, :], set_ps[0:1, 0:NS], -1.0, None, ALU.add))
            dve.wait_ge(setup_products, 2)
            dve.tensor_copy(group_first_step[:, :], set_ps[0:1, 0:NC_G * P])
            dve.wait_ge(setup_done, done)
            setup(dve.tensor_tensor(step_ends[:, 0:NS - 1], step_group[:, 0:NS - 1], step_group[:, 1:NS], ALU.subtract))
            dve.memset(step_ends[:, NS - 1:NS], 1)
            dve.tensor_tensor(step_block[:, :], walk_iota[0:1, :], step_group[:, :], ALU.subtract)
            dve.wait_ge(setup_done, done)
            dve.tensor_scalar(step_ends[:, 0:NS - 1], step_ends[:, 0:NS - 1], 1.0, None, ALU.add)
            dve.tensor_scalar(step_slot[:, :], step_group[:, :], R - 1, None, ALU.bitwise_and).then_inc(walk_ready, 1)

            def measure(half, b, width):
                for k in range(KC):
                    ins = dve.bn_stats(bn_stats[:, k, bass.ds(b * 6 + 6, 6)], half(k)[:, 0:width])
                return ins

            def measure_h(b, par, width):
                dve.wait_ge(transposed, b + (CH + 1))
                measure(lambda k: tr_ps[par][:, k * P:(k + 1) * P], b, width).then_inc(transpose_read, 1)

            def scale_and_shift(which, gamma, beta):
                for k in range(KC):
                    ins = dve.bn_aggr(bn_mv[:, k, :], bn_stats[:, k, 6:(NB + 1) * 6])
                ins.then_inc(bn_step, 1)
                base = which * BN + (which > 0)
                dve.wait_ge(bn_step, base + 1)
                dve.tensor_scalar(bn_var[:, :], bn_mv[:, :, 1], BN_EPS, None, ALU.add).then_inc(bn_step, 1)
                dve.wait_ge(bn_rooted, which + 1)
                inverse_root(bn_rstd[:, :], bn_half[:, :], bn_var[:, :], bn_root[:, :], 3 * (NCH + which), bn_inverted)
                dve.wait_ge(bn_inverted, which + 1)
                dve.tensor_tensor(bn_scale[:, :], bn_rstd[:, :], gamma, ALU.mult).then_inc(bn_step, 1)
                dve.wait_ge(bn_step, base + 3)
                dve.scalar_tensor_tensor(bn_shift[:, :], bn_mv[:, :, 0], -1.0, bn_scale[:, :], ALU.mult, ALU.mult
                                         ).then_inc(bn_fold, 1)
                dve.wait_ge(bn_fold, which + 1)
                dve.tensor_tensor(bn_shift[:, :], bn_shift[:, :], beta, ALU.add).then_inc(bn_step, 1)
                dve.wait_ge(bn_step, base + 4)

            def affine_rows_of_h():
                dve.wait_ge(consts_loaded, 16 * CONST_DMAS)
                dve.wait_ge(transpose_read, NB + 2)
                scale_and_shift(0, vec[:, 0, :], vec[:, 1, :])
                for v, column in enumerate((bn_scale, bn_shift)):
                    for k in range(KC):
                        ins = dve.tensor_scalar(diag[:, v, k, :], ident[:, :], column[:, k:k + 1], None, ALU.mult)
                ins.then_inc(bn_step, 1)
                dve.wait_ge(setup_products, 3)
                dve.tensor_copy(affine_rows[:, :, :].rearrange("p v f -> p (v f)"), set_ps[:, :]).then_inc(setup_done, 1)
                dve.wait_ge(setup_done, done + 1)

            def walk(layer):
                def place(s, par):
                    group = dve.value_load(at(step_group, s), min_val=0, max_val=NG - 1)
                    b = dve.value_load(at(step_block, s), min_val=0, max_val=NB - 1)
                    dve.scalar_tensor_tensor(
                        onehot[:, par, :, :],
                        dst_all[:, bass.ds(group * G, G)].unsqueeze(2).to_broadcast([P, G, P]),
                        block_start[:, bass.ds(b, 1)],
                        iota_row[:, :].unsqueeze(1).to_broadcast([P, G, P]),
                        ALU.subtract, ALU.is_equal).then_inc(onehot_ready, 1)

                def add(s, par):
                    b = dve.value_load(at(step_block, s), min_val=0, max_val=NB - 1)
                    dve.wait_ge(steps_done, s + (layer * NS + 1))
                    dve.wait_ge(sums_added, s + (layer * NS + 2))
                    if layer == 0:
                        dve.tensor_tensor(degree[:, bass.ds(b, 1)], degree[:, bass.ds(b, 1)],
                                          agg_ps[par][:, D:D + 1], ALU.add)
                    dve.tensor_tensor(block_of(b), block_of(b), agg_ps[par][:, 0:D], ALU.add).then_inc(sums_added, 1)

                def end_block(s):
                    ended = dve.value_load(at(step_ends, s), min_val=0, max_val=1)
                    with dve.If(ended == 1):
                        b = dve.value_load(at(step_block, s), min_val=0, max_val=NB - 1)
                        dve.wait_ge(z_kept, b + (layer * NB + 1))
                        measure(lambda k: half_block(b - 1, k), b - 1, P)
                        dve.wait_ge(sums_added, s + (layer * NS + 3))
                        if layer == 0:
                            dve.tensor_tensor(scaled[:, :], block_of(b), affine_rows[:, 0, :], ALU.mult).then_inc(sum_scaled, 1)
                            dve.wait_ge(sum_scaled, b + 1)
                            dve.scalar_tensor_tensor(node_major[:, 0, :], affine_rows[:, 1, :], degree[:, bass.ds(b, 1)],
                                                     scaled[:, :], ALU.mult, ALU.add).then_inc(sum_ready, 1)
                        else:
                            dve.tensor_scalar(node_major[:, 0, :], block_of(b), 1.0, None, ALU.mult).then_inc(sum_ready, 1)

                dve.wait_ge(walk_ready, 1)
                place(0, 0)
                if layer == 0:
                    with dve.Fori(0, EARLY // 2 - 1) as i:
                        for j in range(2):
                            place(i * 2 + (j + 1), 1 - j)
                            for u in range(CH):
                                measure_h(i * (2 * CH) + (j * CH + u), (j * CH + u) % 2, P)
                            add(i * 2 + j, j)
                    for s in range(EARLY - 2, EARLY):
                        place(s + 1, (s + 1) % 2)
                        for b in range(s * CH, (s + 1) * CH):
                            measure_h(b, b % 2, P if b < NB - 1 else LAST)
                        add(s, s % 2)
                    affine_rows_of_h()
                    with dve.Fori(0, EARLY // 2) as i:
                        for j in range(2):
                            place(i * 2 + (EARLY + j + 1), 1 - j)
                            add(i * 2 + (EARLY + j), j)
                            for u in range(2):
                                end_block(i * 4 + (2 * j + u))
                else:
                    with dve.Fori(0, EARLY) as i:
                        for j in range(2):
                            place(i * 2 + (j + 1), 1 - j)
                            add(i * 2 + j, j)
                            end_block(i * 2 + j)
                with dve.Fori(EARLY, NS // 2) as i:
                    for j in range(2):
                        place(i * 2 + (j + 1), 1 - j)
                        add(i * 2 + j, j)
                        end_block(i * 2 + j)
                add(NS - 1, (NS - 1) % 2)
                end_block(NS - 1)
                dve.wait_ge(z_kept, (layer + 1) * NB + 1)
                measure(lambda k: half_block(NB - 1, k), NB - 1, LAST).then_inc(z_measured, 1)

            def dense(layer):
                first = layer * NB

                dve.wait_ge(z_measured, layer + 1)
                scale_and_shift(layer + 1, vec[:, 3 + 3 * layer, :], vec[:, 4 + 3 * layer, :])

                def finish(i, x_odd):
                    for u in range(2 * CH):
                        par, b = u % 2, i * (2 * CH) + u
                        if layer == 1 and u == 0:
                            dve.wait_ge(x_again[0], i * 16 + 16)
                        if layer == 1 and u == CH:
                            dve.wait_ge(x_again[1], x_odd)
                        dve.wait_ge(y_done, b + (first + CH + 1))
                        dve.tensor_tensor(pre_relu[:, par, :], mm_ps[par][:, 0:D], bias_b[layer][:, :], ALU.add
                                          ).then_inc(y_biased, 1)
                        dve.wait_ge(y_biased, b + (first + 3))
                        if layer == 0:
                            dve.tensor_scalar(block_of(b), pre_relu[:, par, :], 0.0, None, ALU.max).then_inc(y_out, 1)
                        else:
                            dve.scalar_tensor_tensor(block_of(b), pre_relu[:, par, :], 0.0, x_slot(u // CH)[:, u % CH, :],
                                                     ALU.max, ALU.add).then_inc(y_out, 1)

                with dve.Fori(0, NCH // 2 - 1) as i:
                    finish(i, i * 16 + 16)
                finish(NCH // 2 - 1, (NCH // 2 + 1) * 16)

            for layer in range(2):
                walk(layer)
                dense(layer)


_INS = ["x", "src", "dst"] + [f"L0_gnn_{n}" for n in
                              ("g0", "b0", "W1a", "b1a", "g1", "bt1", "W1b", "b1b", "W2a", "b2a", "g2", "bt2", "W2b", "b2b")]


def kernel(**inputs):
    import numpy as np
    import concourse.bacc as bacc
    from concourse.bass_utils import run_bass_kernel_spmd

    nc = bacc.Bacc("TRN2", target_bir_lowering=False, num_devices=1)
    arrays, aps = {}, []
    for name in _INS:
        a = np.ascontiguousarray(inputs[name])
        arrays[f"in_{name}"] = a
        aps.append(nc.dram_tensor(f"in_{name}", a.shape, mybir.dt.from_np(a.dtype), kind="ExternalInput").ap())
    out = nc.dram_tensor("out_0", (N, D), F32, kind="ExternalOutput").ap()
    build(nc, *aps, out)
    r = run_bass_kernel_spmd(nc, [arrays], core_ids=[0])
    return r.results[0]["out_0"]
```

```python
from contextlib import ExitStack

import concourse.bass as bass
from concourse import mybir

P = 128
N = 12500
D = 256
E = 212500
KC = D // P
LN_EPS = 1e-5
BN_EPS = 1e-5

NB = (N + P - 1) // P
NPAD = NB * P
LAST = N - (NB - 1) * P
CH = 7
NCH = NB // CH
LB = NCH // 2
NPAIR = NB // 2
G = 8
GE = G * P
NG = (E + GE - 1) // GE
TAIL = E - (NG - 1) * GE
NS = NG + NB - 1
R = 4
RW = 272
NALL = NG * NB
NC_G = (NG + P - 1) // P

assert NB % (2 * CH) == 0 and NG % R == 0 and R & (R - 1) == 0 and TAIL < GE and NG < NC_G * P

F32 = mybir.dt.float32
I32 = mybir.dt.int32
ALU = mybir.AluOpType
ACT = mybir.ActivationFunctionType


def build(nc, x, src, dst, g0, b0, W1a, b1a, g1, bt1, W1b, b1b, W2a, b2a, g2, bt2, W2b, b2b, out):
    tables = [nc.dram_tensor(f"node_rows_{i}", (NPAD, D), F32, kind="Internal").ap() for i in range(2)]
    layers = [(W1a, b1a, g1, bt1, W1b, b1b), (W2a, b2a, g2, bt2, W2b, b2b)]

    ctx = ExitStack()
    with ctx:
        def sb(name, shape, dt=F32):
            return ctx.enter_context(nc.sbuf_tensor(name, shape, dt))

        def pb(name, shape):
            return ctx.enter_context(nc.psum_tensor(name, shape, F32))

        def sem(name):
            return ctx.enter_context(nc.semaphore(name))

        acc = sb("acc", [P, (NB + 1) * D])
        degree = sb("degree", [P, NB])
        rows = sb("rows", [P, R * G * RW])
        dst_int = sb("dst_int", [P, NC_G, GE], I32)
        dst_rows = rows[:, 0:NC_G * GE].rearrange("p (c e) -> p c e", e=GE)
        dst_all = sb("dst_all", [P, NG * G])
        src_stage = sb("src_stage", [P, R * G], I32)
        onehot = sb("onehot", [P, 2, G, P])
        iota_row = sb("iota_row", [P, P])
        part_col = sb("part_col", [P, 1])
        ident = sb("ident", [P, P])
        ones = sb("ones", [P, P])
        block_start = sb("block_start", [P, NB])
        block_starts_next = sb("block_starts_next", [P, NB - 1])
        walk_iota = sb("walk_iota", [P, NS])
        group_no = sb("group_no", [P, NC_G])
        passed = sb("passed", [P, NB - 1])
        first_block = sb("first_block", [P, NC_G])
        group_step = sb("group_step", [P, NC_G])
        group_apart = sb("group_apart", [P, NC_G])
        first_step = sb("first_step", [P, NC_G])
        reached = sb("reached", [P, NC_G, NS])
        step_group = sb("step_group", [1, NS], I32)
        step_block = sb("step_block", [1, NS], I32)
        step_slot = sb("step_slot", [1, NS], I32)
        step_ends = sb("step_ends", [1, NS], I32)
        group_first_step = sb("group_first_step", [1, NC_G * P], I32)
        shift = sb("shift", [P, 2, P])
        disorder = onehot[:, :, :, :].rearrange("p a t c -> p (a t c)")[:, 0:NC_G * GE].rearrange("p (c e) -> p c e", e=GE)
        disorders = sb("disorders", [P, 1])
        unsorted = sb("unsorted", [P, 1])
        is_unsorted = sb("is_unsorted", [1, 1], I32)
        layer_steps = sb("layer_steps", [1, 1], I32)
        w_a = [sb(f"w_a{i}", [P, KC, D]) for i in range(2)]
        w_b = [sb(f"w_b{i}", [P, KC, D]) for i in range(2)]
        vec = sb("vec", [P, 8, KC])
        bias_b = [sb(f"bias_b{i}", [P, D]) for i in range(2)]
        ln_stats = sb("ln_stats", [P, CH, 6])
        ln_mv = sb("ln_mv", [P, LB, CH, 2])
        ln_var = sb("ln_var", [P, LB, CH])
        ln_root = sb("ln_root", [P, LB, CH])
        ln_half = sb("ln_half", [P, CH])
        ln_scale = sb("ln_scale", [P, LB, CH])
        ln_bias = sb("ln_bias", [P, LB, CH])
        bn_stats = sb("bn_stats", [P, KC, (NB + 1) * 6])
        bn_mv = sb("bn_mv", [P, KC, 2])
        bn_rstd = sb("bn_rstd", [P, KC])
        bn_scale = sb("bn_scale", [P, KC])
        bn_shift = sb("bn_shift", [P, KC])
        bn_var = sb("bn_var", [P, KC])
        bn_root = sb("bn_root", [P, KC])
        bn_half = sb("bn_half", [P, KC])
        diag = sb("diag", [P, 2, KC, P])
        affine_rows = sb("affine_rows", [P, 2, D])
        scaled = sb("scaled", [P, D])
        node_major = sb("node_major", [P, CH, D])
        feat_major = sb("feat_major", [P, CH, KC, P])
        pre_relu = sb("pre_relu", [P, 2, D])

        agg_ps = [pb(f"agg_ps{i}", [P, 512]) for i in range(2)]
        tr_ps = [pb(f"tr_ps{i}", [P, 512]) for i in range(2)]
        mm_ps = [pb(f"mm_ps{i}", [P, 512]) for i in range(2)]
        set_ps = pb("set_ps", [P, 512])
        pair_ps = agg_ps + tr_ps + mm_ps + [pb("pair_ps", [P, 512])]

        x_loaded = [sem(f"x_loaded{i}") for i in range(LB)]
        edges_loaded = sem("edges_loaded")
        consts_loaded = sem("consts_loaded")
        pool_consts = sem("pool_consts")
        pool_setup = sem("pool_setup")
        setup_done = sem("setup_done")
        setup_products = sem("setup_products")
        walk_ready = sem("walk_ready")
        ln_step = sem("ln_step")
        waits_passed = sem("waits_passed")
        newton_step = sem("newton_step")
        ln_measured = sem("ln_measured")
        ln_scaled = sem("ln_scaled")
        ln_rooted = sem("ln_rooted")
        bn_rooted = sem("bn_rooted")
        ln_ready = sem("ln_ready")
        h_ready = sem("h_ready")
        table_stored = sem("table_stored")
        src_staged = [sem(f"src_staged{i}") for i in range(R)]
        slot_landed = [sem(f"slot_landed{i}") for i in range(R)]
        groups_ready = sem("groups_ready")
        onehot_ready = sem("onehot_ready")
        steps_done = sem("steps_done")
        sums_added = sem("sums_added")
        node_major_ready = sem("node_major_ready")
        transposed = sem("transposed")
        pair_measured = sem("pair_measured")
        sum_scaled = sem("sum_scaled")
        sum_ready = sem("sum_ready")
        sum_transposed = sem("sum_transposed")
        sum_taken = sem("sum_taken")
        z_done = sem("z_done")
        z_kept = sem("z_kept")
        z_measured = sem("z_measured")
        bn_step = sem("bn_step")
        bn_inverted = sem("bn_inverted")
        bn_fold = sem("bn_fold")
        act_ready = sem("act_ready")
        y_done = sem("y_done")
        y_biased = sem("y_biased")
        y_out = sem("y_out")
        x_again = [sem(f"x_again{i}") for i in range(2)]
        out_stored = sem("out_stored")

        def block_of(b):
            return acc[:, bass.ds(b * D + D, D)]

        def half_block(b, k):
            return acc[:, bass.ds(b * D + (D + k * P), P)]

        def chunk_of(c):
            return acc[:, bass.ds(c * (CH * D) + D, CH * D)].rearrange("p (k f) -> p k f", f=D)

        def dram_chunk(dram, c):
            return dram[bass.ds(c * (CH * P), CH * P), :].rearrange("(k p) f -> p k f", p=P)

        def short_chunk(dram, sbuf):
            first = (NCH - 1) * CH * P
            cut = first + (CH - 1) * P
            return ((dram[first:cut, :].rearrange("(k p) f -> p k f", p=P), sbuf[:, 0:CH - 1, :]),
                    (dram[cut:N, :], sbuf[0:LAST, CH - 1, :]))

        def x_slot(i):
            return rows[:, i * CH * D:(i + 1) * CH * D].rearrange("p (k f) -> p k f", f=D)

        def at(table, i):
            return table[0:1, bass.ds(i, 1)]

        TAIL_DMAS = (TAIL // G > 0) + (TAIL % G > 0)
        EDGE_DMAS = NC_G + 1
        CONST_DMAS = 6 + 8
        BN = 4
        POOL_LOADED = 5
        POOL_SETUP = 6
        SETUP_DISORDERS = 2
        SETUP_ROWS_READ = 2 + NC_G
        SETUP_REACHED = SETUP_ROWS_READ + 5 + NC_G
        SETUP_BANKS_READ = SETUP_REACHED + NC_G * (G // 4) + 2

        block = ctx.enter_context(nc.Block())

        @block.sync
        def _(sp):
            for c in range(LB):
                sp.dma_start(chunk_of(c), dram_chunk(x, c)).then_inc(x_loaded[c], 16)
            sp.wait_ge(pool_consts, 1)
            full, q, r = (NG - 1) * GE, TAIL // G, TAIL % G

            def load_tail(dram, last, done):
                if q:
                    sp.dma_start(last[0:q, :], dram[full:full + q * G].rearrange("(p j) -> p j", j=G)).then_inc(done, 16)
                if r:
                    sp.dma_start(last[q:q + 1, 0:r], dram[full + q * G:E].rearrange("(p j) -> p j", p=1)).then_inc(done, 16)

            for c in range(LB - 1):
                sp.wait_ge(x_loaded[c], 16)
                sp.dma_start(chunk_of(LB + c), dram_chunk(x, LB + c)).then_inc(x_loaded[c], 16)
            sp.wait_ge(x_loaded[LB - 1], 16)
            for dram, sbuf in short_chunk(x, chunk_of(NCH - 1)):
                sp.dma_start(sbuf, dram).then_inc(x_loaded[LB - 1], 16)
            for c in range(NC_G):
                n = min(P, NG - 1 - c * P)
                sp.dma_start(dst_int[0:n, c, :], dst[c * P * GE:(c * P + n) * GE].rearrange("(g e) -> g e", e=GE)
                             ).then_inc(edges_loaded, 16)
            last = (NG - 1) % P
            sp.dma_start(dst_int[last:last + 1, NC_G - 1, 0:TAIL], dst[full:E].rearrange("(g e) -> g e", g=1)
                         ).then_inc(edges_loaded, 16)
            def stage(g, slot):
                sp.dma_start(src_stage[:, slot * G:(slot + 1) * G],
                             src[bass.ds(g * GE, GE)].rearrange("(p j) -> p j", j=G)).then_inc(src_staged[slot], 16)

            def store_rows(t, c, done, count):
                sp.wait_ge(done, count)
                sp.dma_start(dram_chunk(tables[t], c), chunk_of(c)).then_inc(table_stored, 16)

            for slot in range(R):
                stage(slot, slot)
            with sp.Fori(0, NCH) as c:
                store_rows(0, c, h_ready, c + 1)
            for i, (wa, _, _, _, wb, bb) in enumerate(layers):
                sp.dma_start(w_a[i][:, :, :], wa.rearrange("(k p) f -> p k f", p=P)).then_inc(consts_loaded, 16)
                sp.dma_start(w_b[i][:, :, :], wb.rearrange("(k p) f -> p k f", p=P)).then_inc(consts_loaded, 16)
                sp.dma_start(bias_b[i][:, :], bb.partition_broadcast(P)).then_inc(consts_loaded, 16)
            for i, v in enumerate((g0, b0, b1a, g1, bt1, b2a, g2, bt2)):
                sp.dma_start(vec[:, i, :], v.rearrange("(k p) -> p k", p=P),
                             allow_slow_non_contiguous=True).then_inc(consts_loaded, 16)

            def ring(layer):
                def group(i, j, refill):
                    sp.wait_ge(slot_landed[j], i * (16 * G) + (layer * (NG // R) + 1) * 16 * G)
                    sp.sem_inc(groups_ready, 1)
                    if refill:
                        first = sp.value_load(at(group_first_step, i * R + j), min_val=1, max_val=NALL)
                        if layer == 0:
                            sp.wait_ge(steps_done, first)
                        else:
                            sp.wait_ge(steps_done, first + sp.value_load(layer_steps[0:1, 0:1], min_val=NS, max_val=NALL))
                        refill(i, j)

                def usual(i, j):
                    stage(i * R + (j - 1 + R), (j - 1) % R)

                def tail(i, j):
                    load_tail(src, src_stage[:, (R - 1) * G:R * G], src_staged[R - 1])

                for j in range(R):
                    group(0, j, usual if j else None)
                with sp.Fori(1, NG // R - 1) as i:
                    for j in range(R):
                        group(i, j, usual)
                group(NG // R - 1, 0, tail)
                for j in range(1, R):
                    group(NG // R - 1, j, None)

            sp.wait_ge(walk_ready, 1)
            ring(0)
            sp.wait_ge(steps_done, sp.value_load(layer_steps[0:1, 0:1], min_val=NS, max_val=NALL))
            for slot in range(R):
                stage(slot, slot)
            with sp.Fori(0, NCH) as c:
                store_rows(1, c, y_out, c * CH + CH)
            ring(1)
            sp.wait_ge(steps_done, sp.value_load(layer_steps[0:1, 0:1], min_val=NS, max_val=NALL) * 2)

            def load_again(c, i):
                sp.dma_start(x_slot(i), dram_chunk(x, c)).then_inc(x_again[i], 16)

            load_again(0, 0)
            load_again(1, 1)
            with sp.Fori(0, NCH // 2 - 2) as i:
                for j in range(2):
                    sp.wait_ge(y_out, i * (2 * CH) + (NB + (j + 1) * CH))
                    sp.dma_start(dram_chunk(out, i * 2 + j), chunk_of(i * 2 + j)).then_inc(out_stored, 16)
                    load_again(i * 2 + (j + 2), j)
            for c in range(NCH - 4, NCH):
                sp.wait_ge(y_out, NB + (c + 1) * CH)
                if c < NCH - 1:
                    sp.dma_start(dram_chunk(out, c), chunk_of(c)).then_inc(out_stored, 16)
                if c == NCH - 4:
                    load_again(NCH - 2, 0)
                if c == NCH - 3:
                    for dram, sbuf in short_chunk(x, x_slot(1)):
                        sp.dma_start(sbuf, dram).then_inc(x_again[1], 16)
            for dram, sbuf in short_chunk(out, chunk_of(NCH - 1)):
                sp.dma_start(dram, sbuf).then_inc(out_stored, 16)
            sp.wait_ge(out_stored, 16 * (NCH + 1))

        @block.gpsimd
        def _(pool):
            pool.memset(dst_int[:, NC_G - 1, :], NPAD)
            pool.memset(block_of(-1), 0.0)
            pool.memset(block_of(NB - 1), 0.0).then_inc(pool_consts, 1)
            pool.iota(iota_row[:, :], [[1, P]], base=0, channel_multiplier=0, allow_small_or_imprecise_dtypes=True)
            pool.iota(part_col[:, :], [[1, 1]], base=0, channel_multiplier=1, allow_small_or_imprecise_dtypes=True)
            pool.iota(block_start[:, :], [[P, NB]], base=0, channel_multiplier=0, allow_small_or_imprecise_dtypes=True)
            pool.iota(group_no[:, :], [[P, NC_G]], base=0, channel_multiplier=1, allow_small_or_imprecise_dtypes=True)
            pool.iota(walk_iota[:, :], [[1, NS]], base=0, channel_multiplier=0, allow_small_or_imprecise_dtypes=True)
            pool.memset(ones[:, :], 1.0)
            pool.memset(degree[:, :], 1.0).then_inc(pool_consts, 1)

            done = 0

            def setup(ins):
                nonlocal done
                ins.then_inc(pool_setup, 1)
                done += 1

            pool.wait_ge(pool_consts, 2)
            setup(pool.tensor_scalar(ident[:, :], iota_row[:, :], part_col[:, 0:1], None, ALU.is_equal))
            setup(pool.tensor_scalar(shift[:, 0, :], iota_row[:, :], 1.0, part_col[:, 0:1], ALU.add, ALU.is_equal))
            setup(pool.tensor_scalar(shift[:, 1, :], iota_row[:, :], part_col[:, 0:1], float(P - 1), ALU.subtract, ALU.is_equal))
            setup(pool.tensor_scalar(block_starts_next[:, :], block_start[:, 0:NB - 1], float(P), None, ALU.add))
            pool.wait_ge(edges_loaded, 16 * EDGE_DMAS)
            setup(pool.tensor_copy(dst_rows, dst_int[:, :, :]))
            assert done == POOL_LOADED
            pool.wait_ge(pool_setup, done)
            setup(pool.tensor_tensor(disorder[:, :, 0:GE - 1], dst_rows[:, :, 0:GE - 1], dst_rows[:, :, 1:GE], ALU.subtract))
            assert done == POOL_SETUP
            pool.wait_ge(pool_setup, done)
            pool.wait_ge(setup_products, 2)
            pool.wait_ge(setup_done, SETUP_ROWS_READ)
            setup(pool.memset(rows[:, :].rearrange("p (t w) -> p t w", w=RW)[:, :, D:D + 1], 1.0))

            def gather(layer):
                pool.wait_ge(table_stored, 16 * NCH * (layer + 1))
                def slot_of(slot, staged):
                    pool.wait_ge(src_staged[slot], staged)
                    pool.sem_inc(waits_passed, 1)
                    for t in range(slot * G, (slot + 1) * G):
                        pool.indirect_dma_start(
                            rows[:, t * RW:t * RW + D], None, tables[layer][:, :],
                            bass.IndirectOffsetOnAxis(src_stage[:, t:t + 1], 0)).then_inc(slot_landed[slot], 16)

                before = [layer * (NG // R + (TAIL_DMAS - 1 if slot == R - 1 else 0)) * 16 for slot in range(R)]
                with pool.Fori(0, NG // R - 1) as i:
                    for slot in range(R):
                        slot_of(slot, i * 16 + (before[slot] + 16))
                for slot in range(R):
                    slot_of(slot, before[slot] + (NG // R - 1 + (TAIL_DMAS if slot == R - 1 else 1)) * 16)

            gather(0)
            gather(1)

        @block.tensor
        def _(pe):
            pe.sem_inc(transposed, CH)
            pe.sem_inc(y_done, CH)
            pe.wait_ge(pool_setup, POOL_LOADED)
            mm = pe.matmul(set_ps[:, 0:NC_G], shift[:, 0, :], dst_rows[:, :, 0], start=True, stop=(NC_G == 1),
                           skip_group_check=True)
            if NC_G > 1:
                mm = pe.matmul(set_ps[:, 0:NC_G - 1], shift[:, 1, :], dst_rows[:, 1:NC_G, 0], start=False, stop=True,
                               skip_group_check=True)
            mm.then_inc(setup_products, 1)
            for c in range(NC_G):
                for j in range(G):
                    bank = pair_ps[c * (G // 4) + j // 4]
                    mm = pe.transpose(bank[:, (j % 4) * P:(j % 4 + 1) * P], dst_rows[:, c, j:GE:G], ident[:, :])
            mm.then_inc(setup_products, 1)

            pe.wait_ge(setup_done, SETUP_DISORDERS)
            pe.matmul(set_ps[:, 0:1], ones[:, :], disorders[:, :], start=True, stop=True).then_inc(setup_products, 1)
            pe.wait_ge(setup_done, SETUP_REACHED)
            for c in range(NC_G):
                mm = pe.matmul(set_ps[0:1, 0:NS], ones[:, 0:1], reached[:, c, :], start=(c == 0), stop=(c == NC_G - 1))
            mm.then_inc(setup_products, 1)
            for c in range(NC_G):
                mm = pe.matmul(pair_ps[CH - 1][0:1, c * P:(c + 1) * P], first_step[:, c:c + 1], ident[:, :],
                               start=(c == 0), stop=(c == NC_G - 1), skip_group_check=True)
            mm.then_inc(setup_products, 1)

            def transpose_block(n, pair, u):
                pe.wait_ge(node_major_ready, n + 1)
                pe.wait_ge(pair_measured, pair + 1)
                for k in range(KC):
                    at_col = k * 2 * P + (u % 2) * P
                    mm = pe.transpose(pair_ps[u // 2][:, at_col:at_col + P], node_major[:, u % CH, k * P:(k + 1) * P],
                                      ident[:, :])
                mm.then_inc(transposed, 1)

            def affine_to_rows():
                pe.wait_ge(bn_step, BN + 1)
                for v in range(2):
                    for k in range(KC):
                        mm = pe.matmul(set_ps[:, (v * KC + k) * P:(v * KC + k + 1) * P], ones[:, :], diag[:, v, k, :],
                                       start=(v + k == 0), stop=(v + k == KC), skip_group_check=True)
                mm.then_inc(setup_products, 1)

            def walk(layer):
                width = D + 1 if layer == 0 else D

                def sum_group(n, group, par, row_cols):
                    pe.wait_ge(sums_added, n + 1)
                    pe.wait_ge(onehot_ready, n + 1)
                    pe.wait_ge(groups_ready, group + (layer * NG + 1))
                    for t in range(G):
                        mm = pe.matmul(agg_ps[par][:, 0:width], onehot[:, par, t, :], rows[:, row_cols(t)],
                                       start=(t == 0), stop=(t == G - 1))
                    mm.then_inc(steps_done, 1)

                def step(s, par):
                    slot = pe.value_load(at(step_slot, s), min_val=0, max_val=R - 1)
                    group = pe.value_load(at(step_group, s), min_val=0, max_val=NG - 1)
                    sum_group(s + layer * NS, group, par, lambda t: bass.ds(slot * (G * RW) + t * RW, width))

                def end_block(s):
                    ended = pe.value_load(at(step_ends, s - 1), min_val=0, max_val=1)
                    with pe.If(ended == 1):
                        first_product(pe.value_load(at(step_block, s), min_val=1, max_val=NB - 1))

                def first_product(block_done):
                    pe.wait_ge(sum_ready, block_done + layer * NB)
                    for k in range(KC):
                        mm = pe.transpose(tr_ps[0][:, k * P:(k + 1) * P], node_major[:, 0, k * P:(k + 1) * P], ident[:, :])
                    mm.then_inc(sum_transposed, 1)
                    pe.wait_ge(sum_taken, block_done + layer * NB)
                    for o in range(KC):
                        for k in range(KC):
                            mm = pe.matmul(mm_ps[0][:, o * P:(o + 1) * P], w_a[layer][:, k, o * P:(o + 1) * P],
                                           feat_major[:, 0, k, :], start=(o == 0 and k == 0),
                                           stop=(o == KC - 1 and k == KC - 1), skip_group_check=True)
                    mm.then_inc(z_done, 1)

                with pe.If(pe.value_load(is_unsorted[0:1, 0:1], min_val=0, max_val=1) == 0):
                    step(0, 0)
                if layer == 0:
                    affine_to_rows()
                with pe.If(pe.value_load(is_unsorted[0:1, 0:1], min_val=0, max_val=1) == 0):
                    with pe.Fori(0, NS // 2) as i:
                        for j in range(2):
                            step(i * 2 + (j + 1), 1 - j)
                            end_block(i * 2 + (j + 1))
                    first_product(NB)
                with pe.If(pe.value_load(is_unsorted[0:1, 0:1], min_val=0, max_val=1) == 1):
                    with pe.Fori(0, NG // R) as q:
                        for slot in range(R):
                            with pe.Fori(0, NB // 2) as i:
                                for j in range(2):
                                    sum_group(q * (R * NB) + i * 2 + (layer * NALL + slot * NB + j), q * R + slot, j,
                                              lambda t: slice((slot * G + t) * RW, (slot * G + t) * RW + width))
                    with pe.Fori(1, NB + 1) as b:
                        first_product(b)

            def second_product(layer):
                with pe.Fori(0, NB // (2 * CH)) as i:
                    for u in range(2 * CH):
                        par, m = u % 2, i * (2 * CH) + (layer * NB + u)
                        pe.wait_ge(act_ready, m + 1)
                        pe.wait_ge(y_biased, m + 1)
                        for k in range(KC):
                            mm = pe.matmul(mm_ps[par][:, 0:D], feat_major[:, u % CH, k, :], w_b[layer][:, k, :],
                                           start=(k == 0), stop=(k == KC - 1))
                        mm.then_inc(y_done, 1)

            pe.wait_ge(setup_done, SETUP_BANKS_READ)
            with pe.Fori(0, NB // (2 * CH)) as i:
                for u in range(2 * CH):
                    transpose_block(i * (2 * CH) + u, i * CH + u // 2, u)
            pe.wait_ge(consts_loaded, 16 * CONST_DMAS)
            pe.wait_ge(pair_measured, NPAIR - CH + 1 + CH)
            pe.wait_ge(walk_ready, 1)
            pe.wait_ge(pool_setup, POOL_SETUP + 1)
            for layer in range(2):
                walk(layer)
                second_product(layer)

        @block.scalar
        def _(act):
            act.sem_inc(z_kept, 1)

            def copy_block(b, u):
                act.wait_ge(transposed, b + 1)
                act.copy(node_major[:, u % CH, :], block_of(b)).then_inc(node_major_ready, 1)

            def ln_root_of(i, k):
                act.wait_ge(ln_measured, i * LB + (k + 1))
                act.activation(ln_root[:, k, :], ln_var[:, k, :], ACT.Sqrt).then_inc(ln_rooted, 1)

            def normalize(i, k):
                act.wait_ge(ln_ready, i * LB + (k + 1))
                for u in range(CH):
                    b = i * (LB * CH) + (k * CH + u)
                    ins = act.activation(block_of(b), block_of(b), ACT.Relu,
                                         bias=ln_bias[:, k, u:u + 1], scale=ln_scale[:, k, u:u + 1])
                ins.then_inc(h_ready, 1)

            with act.Fori(0, 2) as i:
                for k in range(LB):
                    ln_root_of(i, k)
                    if k:
                        normalize(i, k - 1)
                normalize(i, LB - 1)

            def bn_root_of(which):
                act.wait_ge(bn_step, which * BN + (which > 0) + 2)
                act.activation(bn_root[:, :], bn_var[:, :], ACT.Sqrt).then_inc(bn_rooted, 1)

            act.wait_ge(h_ready, NCH)
            with act.Fori(0, NCH) as c:
                for u in range(CH):
                    copy_block(c * CH + u, u)
            act.wait_ge(consts_loaded, 16 * CONST_DMAS)
            bn_root_of(0)

            def dense(layer):
                bias_a = vec[:, 2 + 3 * layer, :]

                with act.Fori(0, NB) as b:
                    act.wait_ge(sum_transposed, b + (layer * NB + 1))
                    act.copy(feat_major[:, 0, :, :].rearrange("p k f -> p (k f)"), tr_ps[0][:, 0:D]).then_inc(sum_taken, 1)
                    act.wait_ge(z_done, b + (layer * NB + 1))
                    for k in range(KC):
                        ins = act.activation(half_block(b, k), mm_ps[0][:, k * P:(k + 1) * P], ACT.Identity,
                                             bias=bias_a[:, k:k + 1])
                    ins.then_inc(z_kept, 1)
                bn_root_of(layer + 1)
                act.wait_ge(bn_step, (2 + layer) * BN + 1)
                act.wait_ge(z_kept, (layer + 1) * NB + 1)
                with act.Fori(0, NB // (2 * CH)) as i:
                    for u in range(2 * CH):
                        b = i * (2 * CH) + u
                        act.wait_ge(y_done, b + (layer * NB + 1))
                        for k in range(KC):
                            ins = act.activation(feat_major[:, u % CH, k, :], half_block(b, k), ACT.Relu,
                                                 bias=bn_shift[:, k:k + 1], scale=bn_scale[:, k:k + 1])
                        ins.then_inc(act_ready, 1)

            dense(0)
            dense(1)

        @block.vector
        def _(dve):
            dve.sem_inc(sums_added, 2)
            dve.sem_inc(pair_measured, CH)
            dve.sem_inc(y_biased, 2)

            def inverse_root(stage, r, half, var, root, before, done):
                if stage == 0:
                    dve.reciprocal(r, root).then_inc(newton_step, 1)
                if stage == 1:
                    dve.wait_ge(newton_step, before + 1)
                    dve.scalar_tensor_tensor(half, var, -0.5, r, ALU.mult, ALU.mult).then_inc(newton_step, 1)
                if stage == 2:
                    dve.wait_ge(newton_step, before + 2)
                    dve.tensor_tensor(half, half, r, ALU.mult).then_inc(newton_step, 1)
                if stage == 3:
                    dve.wait_ge(newton_step, before + 3)
                    dve.scalar_tensor_tensor(r, half, 1.5, r, ALU.add, ALU.mult).then_inc(done, 1)

            def ln_measure(i, k):
                dve.wait_ge(x_loaded[k], i * (32 if k == LB - 1 else 16) + 16)
                for u in range(CH):
                    ins = dve.bn_stats(ln_stats[:, u, :], block_of(i * (LB * CH) + (k * CH + u)))
                    if k and u >= 1:
                        ln_finish(i, k - 1, u - 1)
                ins.then_inc(ln_step, 1)
                dve.wait_ge(ln_step, i * (2 * LB) + (2 * k + 1))
                dve.sem_inc(waits_passed, 1)
                for u in range(CH):
                    ins = dve.bn_aggr(ln_mv[:, k, u, :], ln_stats[:, u, :])
                ins.then_inc(ln_step, 1)
                dve.wait_ge(ln_step, i * (2 * LB) + (2 * k + 2))
                dve.tensor_scalar(ln_var[:, k, :], ln_mv[:, k, :, 1], LN_EPS, None, ALU.add).then_inc(ln_measured, 1)

            def ln_finish(i, k, stage):
                if stage == 0:
                    dve.wait_ge(ln_rooted, i * LB + (k + 1))
                if stage < 4:
                    inverse_root(stage, ln_scale[:, k, :], ln_half[:, :], ln_var[:, k, :], ln_root[:, k, :],
                                 i * (3 * LB) + 3 * k, ln_scaled)
                if stage == 4:
                    dve.wait_ge(ln_scaled, i * LB + (k + 1))
                    dve.scalar_tensor_tensor(ln_bias[:, k, :], ln_mv[:, k, :, 0], -1.0, ln_scale[:, k, :],
                                             ALU.mult, ALU.mult).then_inc(ln_ready, 1)

            with dve.Fori(0, 2) as i:
                for k in range(LB):
                    ln_measure(i, k)
                for stage in range(5):
                    ln_finish(i, LB - 1, stage)

            done = 0

            def setup(ins):
                nonlocal done
                ins.then_inc(setup_done, 1)
                done += 1

            dve.wait_ge(pool_setup, POOL_SETUP)
            dve.wait_ge(setup_products, 1)
            setup(dve.tensor_tensor(disorder[:, :, GE - 1], dst_rows[:, :, GE - 1], set_ps[:, 0:NC_G], ALU.subtract))
            dve.wait_ge(setup_done, done)
            setup(dve.tensor_scalar(disorder[:, :, :], disorder[:, :, :], 0.0, 0.0, ALU.is_gt, ALU.add,
                                    accum_out=disorders[:, 0:1]))
            assert done == SETUP_DISORDERS
            for c in range(NC_G):
                setup(dve.tensor_scalar(passed[:, :], block_starts_next[:, :], dst_rows[:, c, 0:1], 0.0,
                                        ALU.is_le, ALU.add, accum_out=first_block[:, c:c + 1]))
                dve.wait_ge(setup_done, done)
            assert done == SETUP_ROWS_READ
            setup(dve.scalar_tensor_tensor(group_step[:, :], group_no[:, :], 0.0, first_block[:, :], ALU.is_gt, ALU.mult))
            dve.wait_ge(setup_done, done)
            setup(dve.tensor_tensor(group_step[:, :], group_step[:, :], group_no[:, :], ALU.add))
            dve.wait_ge(setup_products, 3)
            setup(dve.tensor_scalar(unsorted[:, :], set_ps[:, 0:1], 1.5, None, ALU.is_gt))
            dve.wait_ge(setup_done, done)
            setup(dve.scalar_tensor_tensor(group_apart[:, :], group_no[:, :], float(NB), group_step[:, :],
                                           ALU.mult, ALU.subtract))
            dve.wait_ge(setup_done, done)
            setup(dve.scalar_tensor_tensor(first_step[:, :], group_apart[:, :], unsorted[:, 0:1], group_step[:, :],
                                           ALU.mult, ALU.add))
            for c in range(NC_G):
                setup(dve.tensor_scalar(reached[:, c, :], walk_iota[:, :], group_step[:, c:c + 1], None, ALU.is_ge))
            assert done == SETUP_REACHED
            dve.wait_ge(setup_products, 2)
            for c in range(NC_G):
                n = min(P, NG - c * P)
                to = dst_all[:, c * P * G:(c * P + n) * G].rearrange("p (g j) -> p j g", j=G)
                for h in range(G // 4):
                    of = pair_ps[c * (G // 4) + h][:, :].rearrange("p (j g) -> p j g", g=P)
                    setup(dve.tensor_copy(to[:, h * 4:h * 4 + 4, :], of[:, :, 0:n]))
            dve.tensor_copy(is_unsorted[:, :], unsorted[0:1, :])
            dve.tensor_scalar(layer_steps[:, :], unsorted[0:1, :], float(NALL - NS), float(NS), ALU.mult, ALU.add)
            dve.wait_ge(setup_products, 4)
            setup(dve.tensor_scalar(step_group[:, :], set_ps[0:1, 0:NS], -1.0, None, ALU.add))
            dve.wait_ge(setup_products, 5)
            setup(dve.tensor_copy(group_first_step[:, :], pair_ps[CH - 1][0:1, 0:NC_G * P]))
            assert done == SETUP_BANKS_READ
            dve.wait_ge(setup_done, done)
            setup(dve.tensor_tensor(step_ends[:, 0:NS - 1], step_group[:, 0:NS - 1], step_group[:, 1:NS], ALU.subtract))
            dve.memset(step_ends[:, NS - 1:NS], 1)
            dve.tensor_tensor(step_block[:, :], walk_iota[0:1, :], step_group[:, :], ALU.subtract)
            dve.wait_ge(setup_done, done)
            dve.tensor_scalar(step_ends[:, 0:NS - 1], step_ends[:, 0:NS - 1], 1.0, None, ALU.add)
            dve.tensor_scalar(step_slot[:, :], step_group[:, :], R - 1, None, ALU.bitwise_and).then_inc(walk_ready, 1)

            def measure(half, b):
                for k in range(KC):
                    ins = dve.bn_stats(bn_stats[:, k, bass.ds(b * 6 + 6, 6)], half(k))
                return ins

            def measure_pair(pair, bank, width):
                dve.wait_ge(transposed, pair * 2 + (CH + 2))
                measure(lambda k: pair_ps[bank][:, k * 2 * P:k * 2 * P + width], pair).then_inc(pair_measured, 1)

            def scale_and_shift(which, gamma, beta):
                for k in range(KC):
                    ins = dve.bn_aggr(bn_mv[:, k, :], bn_stats[:, k, 6:((NB if which else NPAIR) + 1) * 6])
                ins.then_inc(bn_step, 1)
                base = which * BN + (which > 0)
                dve.wait_ge(bn_step, base + 1)
                dve.tensor_scalar(bn_var[:, :], bn_mv[:, :, 1], BN_EPS, None, ALU.add).then_inc(bn_step, 1)
                dve.wait_ge(bn_rooted, which + 1)
                for stage in range(4):
                    inverse_root(stage, bn_rstd[:, :], bn_half[:, :], bn_var[:, :], bn_root[:, :], 3 * (NCH + which),
                                 bn_inverted)
                dve.wait_ge(bn_inverted, which + 1)
                dve.tensor_tensor(bn_scale[:, :], bn_rstd[:, :], gamma, ALU.mult).then_inc(bn_step, 1)
                dve.wait_ge(bn_step, base + 3)
                dve.scalar_tensor_tensor(bn_shift[:, :], bn_mv[:, :, 0], -1.0, bn_scale[:, :], ALU.mult, ALU.mult
                                         ).then_inc(bn_fold, 1)
                dve.wait_ge(bn_fold, which + 1)
                dve.tensor_tensor(bn_shift[:, :], bn_shift[:, :], beta, ALU.add).then_inc(bn_step, 1)
                dve.wait_ge(bn_step, base + 4)

            def affine_rows_of_h():
                dve.wait_ge(consts_loaded, 16 * CONST_DMAS)
                dve.wait_ge(pair_measured, NPAIR + CH)
                scale_and_shift(0, vec[:, 0, :], vec[:, 1, :])
                for v, column in enumerate((bn_scale, bn_shift)):
                    for k in range(KC):
                        ins = dve.tensor_scalar(diag[:, v, k, :], ident[:, :], column[:, k:k + 1], None, ALU.mult)
                ins.then_inc(bn_step, 1)
                dve.wait_ge(setup_products, 6)
                dve.tensor_copy(affine_rows[:, :, :].rearrange("p v f -> p (v f)"), set_ps[:, :]).then_inc(setup_done, 1)
                dve.wait_ge(setup_done, done + 1)

            def place_group(group, b, par):
                dve.scalar_tensor_tensor(
                    onehot[:, par, :, :],
                    dst_all[:, bass.ds(group * G, G)].unsqueeze(2).to_broadcast([P, G, P]),
                    block_start[:, bass.ds(b, 1)],
                    iota_row[:, :].unsqueeze(1).to_broadcast([P, G, P]),
                    ALU.subtract, ALU.is_equal).then_inc(onehot_ready, 1)

            def place(s, par):
                group = dve.value_load(at(step_group, s), min_val=0, max_val=NG - 1)
                place_group(group, dve.value_load(at(step_block, s), min_val=0, max_val=NB - 1), par)

            def begin_walk():
                with dve.If(dve.value_load(is_unsorted[0:1, 0:1], min_val=0, max_val=1) == 0):
                    place(0, 0)

            def walk(layer):
                def add_sum(n, b, par):
                    dve.wait_ge(steps_done, n + 1)
                    dve.wait_ge(sums_added, n + 2)
                    if layer == 0:
                        dve.tensor_tensor(degree[:, bass.ds(b, 1)], degree[:, bass.ds(b, 1)],
                                          agg_ps[par][:, D:D + 1], ALU.add)
                    dve.tensor_tensor(block_of(b), block_of(b), agg_ps[par][:, 0:D], ALU.add).then_inc(sums_added, 1)

                def hand_over(b):
                    if layer == 0:
                        dve.tensor_tensor(scaled[:, :], block_of(b), affine_rows[:, 0, :], ALU.mult).then_inc(sum_scaled, 1)
                        dve.wait_ge(sum_scaled, b + 1)
                        dve.scalar_tensor_tensor(node_major[:, 0, :], affine_rows[:, 1, :], degree[:, bass.ds(b, 1)],
                                                 scaled[:, :], ALU.mult, ALU.add).then_inc(sum_ready, 1)
                    else:
                        dve.tensor_scalar(node_major[:, 0, :], block_of(b), 1.0, None, ALU.mult).then_inc(sum_ready, 1)

                def measure_before(b):
                    dve.wait_ge(z_kept, b + (layer * NB + 1))
                    measure(lambda k: half_block(b - 1, k), b - 1)

                def add(s, par):
                    add_sum(s + layer * NS, dve.value_load(at(step_block, s), min_val=0, max_val=NB - 1), par)

                def end_block(s):
                    ended = dve.value_load(at(step_ends, s), min_val=0, max_val=1)
                    with dve.If(ended == 1):
                        b = dve.value_load(at(step_block, s), min_val=0, max_val=NB - 1)
                        measure_before(b)
                        dve.wait_ge(sums_added, s + (layer * NS + 3))
                        hand_over(b)

                with dve.If(dve.value_load(is_unsorted[0:1, 0:1], min_val=0, max_val=1) == 0):
                    with dve.Fori(0, NS // 2) as i:
                        for j in range(2):
                            place(i * 2 + (j + 1), 1 - j)
                            add(i * 2 + j, j)
                            end_block(i * 2 + j)
                    add(NS - 1, (NS - 1) % 2)
                    end_block(NS - 1)
                with dve.If(dve.value_load(is_unsorted[0:1, 0:1], min_val=0, max_val=1) == 1):
                    with dve.Fori(0, NG) as g:
                        with dve.Fori(0, NB // 2) as i:
                            for j in range(2):
                                place_group(g, i * 2 + j, j)
                            for j in range(2):
                                add_sum(g * NB + i * 2 + (layer * NALL + j), i * 2 + j, j)
                    dve.wait_ge(sums_added, (layer + 1) * NALL + 2)
                    with dve.Fori(0, NB) as b:
                        measure_before(b)
                        hand_over(b)
                dve.wait_ge(z_kept, (layer + 1) * NB + 1)
                measure(lambda k: half_block(NB - 1, k)[:, 0:LAST], NB - 1).then_inc(z_measured, 1)

            def dense(layer):
                first = layer * NB

                dve.wait_ge(z_measured, layer + 1)
                scale_and_shift(layer + 1, vec[:, 3 + 3 * layer, :], vec[:, 4 + 3 * layer, :])

                def finish(i, x_odd):
                    for u in range(2 * CH):
                        par, b = u % 2, i * (2 * CH) + u
                        if layer == 1 and u == 0:
                            dve.wait_ge(x_again[0], i * 16 + 16)
                        if layer == 1 and u == CH:
                            dve.wait_ge(x_again[1], x_odd)
                        dve.wait_ge(y_done, b + (first + CH + 1))
                        dve.tensor_tensor(pre_relu[:, par, :], mm_ps[par][:, 0:D], bias_b[layer][:, :], ALU.add
                                          ).then_inc(y_biased, 1)
                        dve.wait_ge(y_biased, b + (first + 3))
                        if layer == 0:
                            dve.tensor_scalar(block_of(b), pre_relu[:, par, :], 0.0, None, ALU.max).then_inc(y_out, 1)
                        else:
                            dve.scalar_tensor_tensor(block_of(b), pre_relu[:, par, :], 0.0, x_slot(u // CH)[:, u % CH, :],
                                                     ALU.max, ALU.add).then_inc(y_out, 1)

                with dve.Fori(0, NCH // 2 - 1) as i:
                    finish(i, i * 16 + 16)
                finish(NCH // 2 - 1, (NCH // 2 + 1) * 16)

            dve.wait_ge(walk_ready, 1)
            begin_walk()
            with dve.Fori(0, NPAIR // CH - 1) as i:
                for u in range(CH):
                    measure_pair(i * CH + u, u, 2 * P)
            for u in range(CH):
                measure_pair(NPAIR - CH + u, u, 2 * P if u < CH - 1 else P + LAST)
            affine_rows_of_h()
            for layer in range(2):
                if layer:
                    begin_walk()
                walk(layer)
                dense(layer)


_INS = ["x", "src", "dst"] + [f"L0_gnn_{n}" for n in
                              ("g0", "b0", "W1a", "b1a", "g1", "bt1", "W1b", "b1b", "W2a", "b2a", "g2", "bt2", "W2b", "b2b")]


def kernel(**inputs):
    import numpy as np
    import concourse.bacc as bacc
    from concourse.bass_utils import run_bass_kernel_spmd

    nc = bacc.Bacc("TRN2", target_bir_lowering=False, num_devices=1)
    arrays, aps = {}, []
    for name in _INS:
        a = np.ascontiguousarray(inputs[name])
        arrays[f"in_{name}"] = a
        aps.append(nc.dram_tensor(f"in_{name}", a.shape, mybir.dt.from_np(a.dtype), kind="ExternalInput").ap())
    out = nc.dram_tensor("out_0", (N, D), F32, kind="ExternalOutput").ap()
    build(nc, *aps, out)
    r = run_bass_kernel_spmd(nc, [arrays], core_ids=[0])
    return r.results[0]["out_0"]
```
